# Optimizing a Trainium2 kernel written in Bass

```python
import numpy as np
import jax
import jax.numpy as jnp

def _softmax(x, axis=-1):
    return jax.nn.softmax(x, axis=axis)

def _gelu(x):
    return jax.nn.gelu(x, approximate=True)

def _silu(x):
    return jax.nn.silu(x)

def _sigmoid(x):
    return jax.nn.sigmoid(x)

def _layernorm(x, axis=-1, eps=1e-05):
    m = jnp.mean(x, axis=axis, keepdims=True)
    v = jnp.var(x, axis=axis, keepdims=True)
    return (x - m) / jnp.sqrt(v + eps)

def _scatter_add(tgt, idx, src, axis=0):
    return tgt.at[idx].add(src)

def _segment_sum(src, seg, n):
    return jax.ops.segment_sum(src, seg, n)
kernel_name = 'mk_gps_d2_gnn_r8_ab383b'

def setup_inputs(seed: int=0):
    np.random.seed(seed)
    _w = jnp.asarray

    def _rec_inputs():
        import jax
        import jax.numpy as jnp
        _gk = jax.random.key(seed)
        x = -0.0002117 + 1 * jax.random.normal(jax.random.fold_in(_gk, 1), (1250, 512), jnp.float32)
        _s = jax.random.randint(jax.random.fold_in(_gk, 2), (20000,), 0, 1250, jnp.int32)
        _d = jax.random.randint(jax.random.fold_in(_gk, 3), (20000,), 0, 1250, jnp.int32)
        _loop = jnp.arange(1250, dtype=jnp.int32)
        src = jnp.concatenate([_s, _d, _loop])
        dst = jnp.concatenate([_d, _s, _loop])
        _o = jnp.argsort(dst, stable=True)
        src = src[_o]
        dst = dst[_o]
        edge_weight = jax.random.uniform(jax.random.fold_in(_gk, 13), (41250,), jnp.float32, 0.0, 0.999998)
        return (x, src, dst, edge_weight)
    x, src, dst, edge_weight = _rec_inputs()

    def _L0_gnn_setup():
        import jax, jax.numpy as jnp
        import numpy as np
        N_NODES = 6250
        N_EDGES = 100000
        M_IN = 512
        H_OUT = 512
        key = jax.random.key(seed)
        k1, k2, k3, k4, k5 = jax.random.split(key, 5)
        X = jax.random.normal(k1, (N_NODES, M_IN), dtype=jnp.float32)
        limit = float(np.sqrt(6.0 / (M_IN + H_OUT)))
        W = jax.random.uniform(k2, (M_IN, H_OUT), dtype=jnp.float32, minval=-limit, maxval=limit)
        edge_src = jax.random.randint(k3, (N_EDGES,), 0, N_NODES, dtype=jnp.int64 if jax.config.jax_enable_x64 else jnp.int32)
        edge_dst = jax.random.randint(k4, (N_EDGES,), 0, N_NODES, dtype=jnp.int64 if jax.config.jax_enable_x64 else jnp.int32)
        edge_vals = jax.random.uniform(k5, (N_EDGES,), dtype=jnp.float32, minval=0.0, maxval=1.0)
        return {'X': X, 'W': W, 'edge_src': edge_src, 'edge_dst': edge_dst, 'edge_vals': edge_vals}
    _L0_gnn_all = _L0_gnn_setup()
    _L0_gnn_in = {k: v for k, v in _L0_gnn_all.items() if k in ('W',)}
    del _L0_gnn_all

    def _L0_mix_setup():
        import jax, jax.numpy as jnp
        import numpy as np
        DIM = 512
        HEADS = 8
        DIM_HEAD = 64
        KEY_RATIO = 4
        INNER = HEADS * DIM_HEAD
        B, N = (8, 2048)
        key = jax.random.key(seed)
        ks = jax.random.split(key, 8)
        s_in = 1.0 / np.sqrt(DIM)
        s_h = 1.0 / np.sqrt(DIM_HEAD)
        s_out = 1.0 / np.sqrt(INNER)
        return {'x': jax.random.normal(ks[0], (B, N, DIM), dtype=jnp.float32), 'W_in': jax.random.uniform(ks[1], (DIM, INNER), jnp.float32, -s_in, s_in), 'b_in': jax.random.uniform(ks[2], (INNER,), jnp.float32, -s_in, s_in), 'W_q': jax.random.uniform(ks[3], (DIM_HEAD, KEY_RATIO), jnp.float32, -s_h, s_h), 'W_k': jax.random.uniform(ks[4], (DIM_HEAD, KEY_RATIO), jnp.float32, -s_h, s_h), 'W_v': jax.random.uniform(ks[5], (DIM_HEAD, DIM_HEAD), jnp.float32, -s_h, s_h), 'W_out': jax.random.uniform(ks[6], (INNER, DIM), jnp.float32, -s_out, s_out), 'b_out': jax.random.uniform(ks[7], (DIM,), jnp.float32, -s_out, s_out)}
    _L0_mix_all = _L0_mix_setup()
    _L0_mix_in = {k: v for k, v in _L0_mix_all.items() if k in ('W_in', 'b_in', 'W_q', 'W_k', 'W_v', 'W_out', 'b_out')}
    del _L0_mix_all

    def _L0_ffn_setup():
        import jax, jax.numpy as jnp
        import numpy as np
        B, T, D = (4, 1024, 512)
        E, F, CAP = (8, 256, 512)
        key = jax.random.key(seed)
        ks = jax.random.split(key, 6)
        s = 0.02
        return {'x': jax.random.normal(ks[0], (B, T, D), dtype=jnp.float32), 'Wr': jax.random.normal(ks[1], (D, E), dtype=jnp.float32) * s, 'W1': jax.random.normal(ks[2], (E, D, F), dtype=jnp.float32) * s, 'b1': jax.random.normal(ks[3], (E, F), dtype=jnp.float32) * s, 'W2': jax.random.normal(ks[4], (E, F, D), dtype=jnp.float32) * s, 'b2': jax.random.normal(ks[5], (E, D), dtype=jnp.float32) * s}
    _L0_ffn_all = _L0_ffn_setup()
    _L0_ffn_in = {k: v for k, v in _L0_ffn_all.items() if k in ('Wr', 'W1', 'b1', 'W2', 'b2')}
    del _L0_ffn_all

    def _L1_gnn_setup():
        import jax, jax.numpy as jnp
        import numpy as np
        N = 6250
        DIM = 512
        E = 18750
        key = jax.random.key(seed)
        k_x, k_src, k_dst, k_w, k_b = jax.random.split(key, 5)
        x = jax.random.normal(k_x, (N, DIM), dtype=jnp.float32)
        src = jax.random.randint(k_src, (E,), 0, N)
        dst = jax.random.randint(k_dst, (E,), 0, N)
        edge_index = jnp.stack([src, dst], axis=0)
        bound = 1.0 / np.sqrt(DIM)
        W = jax.random.uniform(k_w, (DIM, DIM), minval=-bound, maxval=bound, dtype=jnp.float32)
        b = jax.random.uniform(k_b, (DIM,), minval=-bound, maxval=bound, dtype=jnp.float32)
        alpha = jnp.float32(0.5)
        return {'x': x, 'edge_index': edge_index, 'num_nodes': N, 'alpha': alpha, 'W': W, 'b': b}
    _L1_gnn_all = _L1_gnn_setup()
    _L1_gnn_in = {k: v for k, v in _L1_gnn_all.items() if k in ('alpha', 'W', 'b')}
    del _L1_gnn_all

    def _L1_mix_setup():
        import jax, jax.numpy as jnp
        import numpy as np
        EPS = 1e-05

        def gamma_layer_norm(x, gamma):
            mu = jnp.mean(x, axis=-1, keepdims=True)
            var = jnp.var(x, axis=-1, keepdims=True)
            return (x - mu) * jax.lax.rsqrt(var + EPS) * gamma
        key = jax.random.key(seed)
        k1, k2, k3, k4 = jax.random.split(key, 4)
        b, n, dim = (8, 512, 512)
        heads, head_size = (8, 64)
        hidden = heads * head_size
        x = jax.random.normal(k1, (b, n, dim), dtype=jnp.float32)
        w_qkv = jax.random.normal(k2, (3 * hidden, dim), dtype=jnp.float32) * dim ** (-0.5)
        w_out = jax.random.normal(k3, (dim, hidden), dtype=jnp.float32) * hidden ** (-0.5)
        gamma = 1.0 + 0.02 * jax.random.normal(k4, (dim,), dtype=jnp.float32)
        return {'x': x, 'w_qkv': w_qkv, 'w_out': w_out, 'gamma': gamma}
    _L1_mix_all = _L1_mix_setup()
    _L1_mix_in = {k: v for k, v in _L1_mix_all.items() if k in ('w_qkv', 'w_out', 'gamma')}
    del _L1_mix_all

    def _L1_ffn_setup():
        import jax, jax.numpy as jnp
        import numpy as np
        from jax import lax
        N_HEADS = 8
        D_KEYS = 128
        HALF = D_KEYS // 2
        N_KEYS = 256
        TOP_K = 8
        D_MODEL = 512

        def _forward(queries, Wq, bq, keys, w_down, w_up):
            N, T, D = queries.shape
            x = queries.reshape(-1, D)
            q = (x @ Wq + bq).reshape(-1, N_HEADS, D_KEYS)
            q1, q2 = (q[..., :HALF], q[..., HALF:])
            s1 = jnp.einsum('bhc,hnc->bhn', q1, keys[:, 0])
            s2 = jnp.einsum('bhc,hnc->bhn', q2, keys[:, 1])
            s1t, i1 = lax.top_k(s1, TOP_K)
            s2t, i2 = lax.top_k(s2, TOP_K)
            all_scores = (s1t[..., :, None] + s2t[..., None, :]).reshape(-1, N_HEADS, TOP_K * TOP_K)
            all_idx = (i1[..., :, None] * N_KEYS + i2[..., None, :]).reshape(-1, N_HEADS, TOP_K * TOP_K)
            scores, best = lax.top_k(all_scores, TOP_K)
            indices = jnp.take_along_axis(all_idx, best, axis=-1)
            w_d = w_down[indices]
            w_u = w_up[indices]
            inner = jnp.einsum('bd,bhkd->bhk', x, w_d)
            vals = jax.nn.relu(inner) * jax.nn.softmax(scores, axis=-1)
            out = jnp.einsum('bhk,bhkd->bd', vals, w_u)
            return out.reshape(N, T, D)
        key = jax.random.key(seed)
        ks = jax.random.split(key, 6)
        N, T = (2, 1024)
        queries = jax.random.normal(ks[0], (N, T, D_MODEL), dtype=jnp.float32)
        Wq = jax.random.normal(ks[1], (D_MODEL, N_HEADS * D_KEYS), dtype=jnp.float32) / np.sqrt(D_MODEL)
        bq = jnp.zeros((N_HEADS * D_KEYS,), dtype=jnp.float32)
        bound = 1.0 / np.sqrt(HALF)
        keys = jax.random.uniform(ks[2], (N_HEADS, 2, N_KEYS, HALF), dtype=jnp.float32, minval=-bound, maxval=bound)
        w_down = jax.random.normal(ks[3], (N_KEYS * N_KEYS, D_MODEL), dtype=jnp.float32) * 0.02
        w_up = jax.random.normal(ks[4], (N_KEYS * N_KEYS, D_MODEL), dtype=jnp.float32) * 0.02
        return {'queries': queries, 'Wq': Wq, 'bq': bq, 'keys': keys, 'w_down': w_down, 'w_up': w_up}
    _L1_ffn_all = _L1_ffn_setup()
    _L1_ffn_in = {k: v for k, v in _L1_ffn_all.items() if k in ('Wq', 'bq', 'keys', 'w_down', 'w_up')}
    del _L1_ffn_all
    return {'x': x, 'src': src, 'dst': dst, 'edge_weight': edge_weight, 'L0_gnn_W': _L0_gnn_in['W'], 'L0_mix_W_in': _L0_mix_in['W_in'], 'L0_mix_b_in': _L0_mix_in['b_in'], 'L0_mix_W_q': _L0_mix_in['W_q'], 'L0_mix_W_k': _L0_mix_in['W_k'], 'L0_mix_W_v': _L0_mix_in['W_v'], 'L0_mix_W_out': _L0_mix_in['W_out'], 'L0_mix_b_out': _L0_mix_in['b_out'], 'L0_ffn_Wr': _L0_ffn_in['Wr'], 'L0_ffn_W1': _L0_ffn_in['W1'], 'L0_ffn_b1': _L0_ffn_in['b1'], 'L0_ffn_W2': _L0_ffn_in['W2'], 'L0_ffn_b2': _L0_ffn_in['b2'], 'L1_gnn_alpha': _L1_gnn_in['alpha'], 'L1_gnn_W': _L1_gnn_in['W'], 'L1_gnn_b': _L1_gnn_in['b'], 'L1_mix_w_qkv': _L1_mix_in['w_qkv'], 'L1_mix_w_out': _L1_mix_in['w_out'], 'L1_mix_gamma': _L1_mix_in['gamma'], 'L1_ffn_Wq': _L1_ffn_in['Wq'], 'L1_ffn_bq': _L1_ffn_in['bq'], 'L1_ffn_keys': _L1_ffn_in['keys'], 'L1_ffn_w_down': _L1_ffn_in['w_down'], 'L1_ffn_w_up': _L1_ffn_in['w_up']}

def reference(x, src, dst, edge_weight, L0_gnn_W, L0_mix_W_in, L0_mix_b_in, L0_mix_W_q, L0_mix_W_k, L0_mix_W_v, L0_mix_W_out, L0_mix_b_out, L0_ffn_Wr, L0_ffn_W1, L0_ffn_b1, L0_ffn_W2, L0_ffn_b2, L1_gnn_alpha, L1_gnn_W, L1_gnn_b, L1_mix_w_qkv, L1_mix_w_out, L1_mix_gamma, L1_ffn_Wq, L1_ffn_bq, L1_ffn_keys, L1_ffn_w_down, L1_ffn_w_up):
    import jax
    import jax.numpy as jnp

    def _L0_gnn_ref(X, W, edge_src, edge_dst, edge_vals):
        import jax, jax.numpy as jnp
        import numpy as np
        N_NODES = 6250
        N_EDGES = 100000
        M_IN = 512
        H_OUT = 512
        Z = jnp.matmul(X, W)
        msg = Z[edge_src] * edge_vals[:, None]
        agg = jax.ops.segment_sum(msg, edge_dst, num_segments=X.shape[0])
        return jax.nn.relu(agg)

    def _L0_mix_ref(x, W_in, b_in, W_q, W_k, W_v, W_out, b_out):
        import jax, jax.numpy as jnp
        import numpy as np
        DIM = 512
        HEADS = 8
        DIM_HEAD = 64
        KEY_RATIO = 4
        INNER = HEADS * DIM_HEAD
        B, N = (8, 2048)
        Bx, Nx, _ = x.shape
        x_mid = x @ W_in + b_in
        x_mid = x_mid.reshape(Bx, Nx, HEADS, DIM_HEAD).transpose(0, 2, 1, 3)
        q = jnp.einsum('bhnd,dr->bhnr', x_mid, W_q)
        k = jnp.einsum('bhnd,dr->bhnr', x_mid, W_k)
        v = jnp.einsum('bhnd,dc->bhnc', x_mid, W_v)
        q = jax.nn.softmax(q, axis=-1)
        k = jax.nn.softmax(k, axis=-2)
        kv = jnp.einsum('bhnr,bhnc->bhrc', k, v)
        qkv = jnp.einsum('bhnr,bhrc->bhnc', q, kv)
        qkv = qkv.transpose(0, 2, 1, 3).reshape(Bx, Nx, INNER)
        return qkv @ W_out + b_out

    def _L0_ffn_ref(x, Wr, W1, b1, W2, b2):
        import jax, jax.numpy as jnp
        import numpy as np
        B, T, D = (4, 1024, 512)
        E, F, CAP = (8, 256, 512)
        Bb, Tt, Dd = x.shape
        N = Bb * Tt
        C = min(CAP, N)
        x_flat = x.reshape(N, Dd)
        logits = x_flat @ Wr
        probs = jax.nn.softmax(logits, axis=0)
        vals, idx = jax.lax.top_k(probs.T, C)
        selected = x_flat[idx]
        h = jax.nn.gelu(jnp.einsum('ecd,edf->ecf', selected, W1) + b1[:, None, :], approximate=False)
        out_e = jnp.einsum('ecf,efd->ecd', h, W2) + b2[:, None, :]
        weighted = vals[..., None] * out_e
        output = jnp.zeros_like(x_flat).at[idx.reshape(-1)].add(weighted.reshape(-1, Dd))
        return output.reshape(Bb, Tt, Dd)

    def _L1_gnn_ref(x, edge_index, num_nodes, alpha, W, b):
        import jax, jax.numpy as jnp
        import numpy as np
        N = 6250
        DIM = 512
        E = 18750
        src = edge_index[0]
        dst = edge_index[1]
        agg = jax.ops.segment_sum(x[src], dst, num_segments=num_nodes)
        deg = jax.ops.segment_sum(jnp.ones_like(dst, dtype=x.dtype), dst, num_segments=num_nodes)
        deg = jnp.maximum(deg, 1.0)
        agg = agg / deg[:, None]
        return x + alpha * (agg @ W.T + b)

    def _L1_mix_ref(x, w_qkv, w_out, gamma):
        import jax, jax.numpy as jnp
        import numpy as np
        EPS = 1e-05

        def gamma_layer_norm(x, gamma):
            mu = jnp.mean(x, axis=-1, keepdims=True)
            var = jnp.var(x, axis=-1, keepdims=True)
            return (x - mu) * jax.lax.rsqrt(var + EPS) * gamma
        b, n, dim = x.shape
        heads, head_size = (8, 64)
        scale = head_size ** (-0.5)
        qkv = jnp.einsum('bnd,hd->bnh', x, w_qkv)
        q, k, v = jnp.split(qkv, 3, axis=-1)

        def to_heads(t):
            return t.reshape(b, n, heads, head_size).transpose(0, 2, 1, 3)
        q, k, v = (to_heads(q), to_heads(k), to_heads(v))
        q = jax.nn.softmax(q, axis=-1) * scale
        k = jax.nn.softmax(k, axis=-2)
        context = jnp.einsum('bhnd,bhne->bhde', k, v)
        out = jnp.einsum('bhde,bhnd->bhne', context, q)
        out = out.transpose(0, 2, 1, 3).reshape(b, n, heads * head_size)
        out = jnp.einsum('bnh,dh->bnd', out, w_out)
        out = gamma_layer_norm(out, gamma)
        return out

    def _L1_ffn_ref(queries, Wq, bq, keys, w_down, w_up):
        import jax, jax.numpy as jnp
        import numpy as np
        from jax import lax
        N_HEADS = 8
        D_KEYS = 128
        HALF = D_KEYS // 2
        N_KEYS = 256
        TOP_K = 8
        D_MODEL = 512

        def _forward(queries, Wq, bq, keys, w_down, w_up):
            N, T, D = queries.shape
            x = queries.reshape(-1, D)
            q = (x @ Wq + bq).reshape(-1, N_HEADS, D_KEYS)
            q1, q2 = (q[..., :HALF], q[..., HALF:])
            s1 = jnp.einsum('bhc,hnc->bhn', q1, keys[:, 0])
            s2 = jnp.einsum('bhc,hnc->bhn', q2, keys[:, 1])
            s1t, i1 = lax.top_k(s1, TOP_K)
            s2t, i2 = lax.top_k(s2, TOP_K)
            all_scores = (s1t[..., :, None] + s2t[..., None, :]).reshape(-1, N_HEADS, TOP_K * TOP_K)
            all_idx = (i1[..., :, None] * N_KEYS + i2[..., None, :]).reshape(-1, N_HEADS, TOP_K * TOP_K)
            scores, best = lax.top_k(all_scores, TOP_K)
            indices = jnp.take_along_axis(all_idx, best, axis=-1)
            w_d = w_down[indices]
            w_u = w_up[indices]
            inner = jnp.einsum('bd,bhkd->bhk', x, w_d)
            vals = jax.nn.relu(inner) * jax.nn.softmax(scores, axis=-1)
            out = jnp.einsum('bhk,bhkd->bd', vals, w_u)
            return out.reshape(N, T, D)
        return _forward(queries, Wq, bq, keys, w_down, w_up)
    edge_index = jnp.stack([src, dst])
    xn = _layernorm(x, axis=-1)
    x = x + _L0_gnn_ref(xn, L0_gnn_W, src, dst, edge_weight) + _L0_mix_ref(xn[None], L0_mix_W_in, L0_mix_b_in, L0_mix_W_q, L0_mix_W_k, L0_mix_W_v, L0_mix_W_out, L0_mix_b_out)[0]
    x = x + _L0_ffn_ref(_layernorm(x, axis=-1)[None], L0_ffn_Wr, L0_ffn_W1, L0_ffn_b1, L0_ffn_W2, L0_ffn_b2)[0]
    xn = _layernorm(x, axis=-1)
    x = x + _L1_gnn_ref(xn, edge_index, 1250, L1_gnn_alpha, L1_gnn_W, L1_gnn_b) + _L1_mix_ref(xn[None], L1_mix_w_qkv, L1_mix_w_out, L1_mix_gamma)[0]
    x = x + _L1_ffn_ref(_layernorm(x, axis=-1)[None], L1_ffn_Wq, L1_ffn_bq, L1_ffn_keys, L1_ffn_w_down, L1_ffn_w_up)[0]
    return x

_drawn_inputs = setup_inputs


def setup_inputs(seed=0):
    import zlib

    import numpy as np

    out = dict(_drawn_inputs(seed))
    spreads = {'L1_ffn_bq': (0.0, 2.0)}
    factors = {'L0_mix_W_in': 8.0,
     'L0_mix_b_in': 8.0,
     'L0_mix_W_q': 8.0,
     'L0_mix_W_k': 8.0,
     'L0_mix_W_v': 8.0,
     'L0_mix_W_out': 7.582,
     'L0_mix_b_out': 28.392,
     'L0_ffn_Wr': 64.0,
     'L0_ffn_W1': 64.0,
     'L0_ffn_b1': 200.0,
     'L0_ffn_W2': 64.0,
     'L0_ffn_b2': 200.0,
     'L1_gnn_W': 23.984,
     'L1_gnn_b': 64.0,
     'L1_mix_gamma': 64.0,
     'L1_ffn_Wq': 41.082,
     'L1_ffn_keys': 40.912,
     'L1_ffn_w_down': 48.781,
     'L1_ffn_w_up': 40.617,
     'edge_weight': 4.999,
     'L0_gnn_W': 2.761}
    for name, (base, spread) in spreads.items():
        noise = np.random.default_rng([zlib.crc32(name.encode()), seed]).standard_normal(out[name].shape)
        drawn = base * np.exp(spread * noise) if base else spread * noise
        out[name] = jnp.asarray(drawn.astype(out[name].dtype))
    for name, factor in factors.items():
        out[name] = (out[name] * factor).astype(out[name].dtype)
    return out
```

```python
import concourse.bass as bass
from concourse import mybir
from contextlib import ExitStack

F32 = mybir.dt.float32
BF16 = mybir.dt.bfloat16
I32 = mybir.dt.int32
U32 = mybir.dt.uint32
I16 = mybir.dt.int16
U16 = mybir.dt.uint16
ALU = mybir.AluOpType
ACT = mybir.ActivationFunctionType
AX = mybir.AxisListType
ds = bass.ds

N = 1250
D = 512
P = 128
T = (N + P - 1) // P
NP = T * P
TAIL = N - (T - 1) * P
KD = D // P
CHUNKS = [(0, 512), (512, 512), (1024, 256)]
EDGES = 41250
NB = (EDGES + P - 1) // P
NBP = 3 * P
WIN = 32
NW = NP // WIN
OHB = 3
NBE = NB + OHB - 1
NBV = NBE + OHB - 1
TURNS = (NB + OHB - 1) // OHB
FIRST_BITS, TURN_BITS = 9, 7
assert NB <= 1 << FIRST_BITS and TURNS < 1 << TURN_BITS and TURNS * NW < 1 << 30 - FIRST_BITS - TURN_BITS
HEADS = 8
KR = 4
HR = HEADS * KR
NE = 8
FF = 256
FB = FF // P
CAP = 512
ROUNDS = 8
PH = 8
NK = 256
TK = 8
GPT = PH * TK
SLOTS = 16
EPS = 1e-5
CONSTANTS = 18


class Chain:

    def __init__(self, engine, sem):
        self.engine, self.sem, self.n, self.base = engine, sem, 0, 0

    def __call__(self, instruction):
        instruction.then_inc(self.sem, 1)
        self.n += 1
        self.engine.wait_ge(self.sem, self.base + self.n)


    def enter(self, turn, links):
        self.outer = self.base + self.n
        self.base, self.n = self.outer + turn * links, 0
        self.links = links

    def leave(self, turns):
        assert self.n == self.links
        self.base, self.n = self.outer + turns * self.links, 0


def gps_two_layers(nc, d, out, last_stage):
    ctx = ExitStack()
    with ctx:
        def sb(name, shape, dt=F32):
            return ctx.enter_context(nc.sbuf_tensor(name, shape, dt))

        def sem(name):
            return ctx.enter_context(nc.semaphore(name))

        X = sb("X", [P, T * D])
        XN = sb("XN", [P, T * D])
        XNT = sb("XNT", [P, KD * NP])
        XNT3 = XNT[:, :].rearrange("p (i n) -> p i n", i=KD)
        ARENA = sb("ARENA", [P, 5120 + 12800 + 6400])
        ZF = ARENA[:, 0:5120]
        A0 = ARENA[:, 5120:17920]
        A1C = ARENA[:, 17920:24320].bitcast(U16)
        WREG = sb("WREG", [P, 10240])
        edgef = sb("edgef", [P, 2 * NBP])
        dstf = edgef[:, 0:NBP]
        srcf = edgef[:, NBP:2 * NBP]
        iota32 = sb("iota32", [P, WIN])
        windows = sb("windows", [P, NW])
        wparts = sb("wparts", [P, NBP * 4], BF16)
        ident = sb("ident", [P, P])
        ones = sb("ones", [P, P])
        iota16 = sb("iota16", [P, NP], I16)
        small = sb("small", [P, 768])
        epsc = small[:, 0:1]
        stat = small[:, 8:68]
        mv = small[:, 68:88]
        rstd = small[:, 88:98]
        rstd2 = small[:, 98:108]
        degc = small[:, 108:118]
        adeg = small[:, 118:128]
        PS = ctx.enter_context(nc.psum_tensor("PS", [P, 4096], F32))

        def bank(b, n=512, p=P, start=0):
            return PS[0:p, 512 * b + start:512 * b + start + n]

        raw_dst = A0[:, 0:NBP].bitcast(I32)
        raw_src = A0[:, NBP:2 * NBP].bitcast(I32)
        raw_w = A0[:, 2 * NBP:3 * NBP]
        res1 = A0[:, 3 * NBP:4 * NBP]
        dmin = A0[:, 4 * NBP:5 * NBP]
        dmax = A0[:, 5 * NBP:6 * NBP]
        hit = A0[0:NW, 6 * NBP:7 * NBP]
        hitb = A0[0:NW, 7 * NBP:8 * NBP]
        bup = A0[0:NW, 8 * NBP:9 * NBP]
        bdown = A0[0:NW, 9 * NBP:10 * NBP]
        bthird = A0[0:NW, 10 * NBP:11 * NBP]
        flat3 = A0[0:NW, 11 * NBP:11 * NBP + 3 * NW]
        dlow = A0[:, 11 * NBP + 3 * NW:12 * NBP + 3 * NW]
        dtmp = A0[:, 12 * NBP + 3 * NW:13 * NBP + 3 * NW].bitcast(I32)
        blkmin = small[:, 128:131]
        blkmax = small[:, 131:134]
        winlo = small[0:NW, 134:135]
        winhi = small[0:NW, 135:136]
        wfirst = small[0:NW, 136:137]
        wend = small[0:NW, 137:138]
        woff = small[0:NW, 138:139]
        wcnt = small[0:NW, 139:140]
        tri = small[0:NW, 140:140 + NW]
        bounds3 = small[0:1, 180:180 + 3 * NW].bitcast(I32)
        bounds = small[0:1, 520:520 + NW].bitcast(I32)
        W0 = WREG[:, 0:2048]
        Win = WREG[:, 2048:4096]
        WinT = WREG[:, 4096:6144]
        Wout = WREG[:, 6144:8192]
        VO = WREG[:, 8192:10240]
        q0 = 5376
        WF = A0[:, q0:q0 + 256]
        bdqk = A0[:, q0 + 256:q0 + 272]
        bdv = A0[:, q0 + 272:q0 + 400]
        binc = A0[:, q0 + 400:q0 + 404]
        qkb = A0[0:1, q0 + 404:q0 + 468]
        headmask = A0[0:HR, q0 + 500:q0 + 1012]
        qrow = A0[:, q0 + 1012:q0 + 1332]
        krow = A0[:, q0 + 1332:q0 + 1652]
        qmax = A0[:, q0 + 1652:q0 + 1732]
        kxT = A0[:, q0 + 1732:q0 + 1860]
        kxm = A0[0:HR, q0 + 1860:q0 + 2372]
        kxmT = A0[:, q0 + 2372:q0 + 2500]
        Mx = A0[0:HR, q0 + 2500:q0 + 3012]
        kTe = A0[0:HR, q0 + 3012:q0 + 3012 + NP]
        qTs = A0[0:HR, q0 + 4300:q0 + 4300 + NP]
        boutr = A0[0:1, q0 + 5600:q0 + 6112]
        binr = A0[0:1, q0 + 6112:q0 + 6624]
        ksum = small[0:HR, 320:321]
        kneg = small[0:HR, 321:322]
        ohs = [XNT[:, 640 * k:640 * k + 640].bitcast(BF16) for k in range(OHB)]
        ohd = [XNT[:, 1920 + 64 * k:1984 + 64 * k].bitcast(BF16) for k in range(OHB)]
        zero_b = XNT[:, 2112:2112 + 64].bitcast(BF16)
        staged = XNT[:, 2176:2176 + 2 * 960]
        summed = XNT[:, 4096:4096 + 2 * 320]
        inwin = XNT[:, 4736:4736 + NBV]
        dwin = XN[:, 0:NBP]
        eq32 = WREG[:, 4096:4096 + NBV * WIN // 2].bitcast(BF16)
        EW = [WREG[:, 0:2048], WREG[:, 2048:4096]]
        hT = [ZF[:, 0:2560], ZF[:, 2560:5120]]
        prob = WREG[0:NE, 4096:5376]
        probR = WREG[:, 5376:6656]
        sel1 = WREG[:, 6656:7936]
        sel2 = WREG[:, 7936:9216]
        b2 = WREG[0:NE, 9312:9824]
        wr = WREG[:, 9824:9856]
        b1k = [WREG[:, 9856:9858], WREG[:, 9858:9860]]
        gate = WREG[:, 9860:9940]
        esame = WREG[:, 9940:10068]
        erep = WREG[0:NE, 10068:10196]
        jbits = small[:, 330:330 + ROUNDS].bitcast(I32)
        jcol = small[:, 340:341].bitcast(I32)
        jcl = small[:, 341:342].bitcast(I32)
        basei = small[:, 342:343].bitcast(I32)
        thri = small[:, 343:344].bitcast(I32)
        thrf = small[:, 343:344]
        cntc = small[:, 344:345]
        okc = small[:, 345:346]
        stepf = small[:, 346:347]
        stepi = small[:, 347:348].bitcast(I32)
        pneg = small[0:NE, 348:349]
        psumc = small[0:NE, 349:350]
        cgt = small[0:NE, 350:351]
        need = small[0:NE, 351:352]
        Wqkv = WREG[:, 4096:10240]
        Wg1 = WREG[:, 0:2048]
        Wo1 = WREG[:, 2048:4096]
        kT1 = A0[:, 0:5120]
        kR1 = A0[:, 5120:10240]
        ctxT = A0[:, 10240:10752]
        M1 = A0[:, 10752:12800]
        QR = ARENA[:, 17920:23040]
        bmask = ARENA[:, 23040:23168]
        qT1 = kT1
        MO = kR1
        V1 = ZF
        gam = ARENA[:, 23168:23680]
        ab = ARENA[:, 23680:24192]
        kneg1 = small[:, 360:364]
        ksum1 = small[:, 364:368]
        alphac = small[:, 368:369]
        a1sum = QR[:, 0:NP]
        qm1 = small[:, 384:464]
        gamr = wparts[0:1, 0:1024].bitcast(F32)
        br1 = edgef[0:1, 0:D]
        alr = small[0:1, 369:370]
        Wq4 = WREG[:, 0:4096]
        keysT = WREG[:, 4096:6144]
        qT4 = WREG[:, 6144:7168]
        s8 = WREG[:, 7168:7296]
        i8 = WREG[:, 7296:7424].bitcast(U32)
        i8f = WREG[:, 7424:7552]
        comb = WREG[:, 7552:8064]
        v8 = WREG[:, 8064:8128]
        pos = WREG[:, 8128:8192].bitcast(U32)
        posa = WREG[:, 8192:8256].bitcast(U32)
        posb = WREG[:, 8256:8320].bitcast(U32)
        posf = WREG[:, 8320:8448]
        eqk = WREG[:, 8448:8960]
        isel = WREG[:, 8960:9088]
        rowid = [WREG[:, 9088 + 64 * k:9152 + 64 * k].bitcast(I32) for k in range(2)]
        soft = [WREG[:, 9216 + 64 * k:9280 + 64 * k] for k in range(2)]
        inner = WREG[:, 9344:9408]
        vals = WREG[:, 9408:9472]
        xcur = [ARENA[:, 16896 + 512 * k:17408 + 512 * k] for k in range(2)]
        diag = [ARENA[:, 17920 + 128 * k:18048 + 128 * k] for k in range(4)]
        slot = [ARENA[:, 1024 * k:1024 * k + 1024] for k in range(SLOTS)]
        iota8 = small[:, 470:478]
        bq4 = small[:, 480:488]
        smax = small[:, 488:496]
        scale2 = small[:, 500:500 + ROUNDS]

        s_x = sem("x_loaded")
        s_edges = sem("edges_loaded")
        s_w0 = sem("layer0_weights_loaded")
        s_const = sem("constants_built")
        s_dv = sem("vector_chain")
        s_sc = sem("scalar_chain")
        s_po = sem("window_parts_added")
        s_po2 = sem("masks_built")
        stage_end = [sem(f"stage_{k}_ended") for k in range(8)]
        s_var = [sem(f"variance_ready_{l}") for l in range(4)]
        s_sd = [sem(f"deviation_ready_{l}") for l in range(4)]
        s_xn = [sem(f"norm_ready_{l}") for l in range(4)]
        s_xtp = [sem(f"norm_transposed_{l}") for l in range(4)]
        s_xt = [sem(f"norm_transpose_copied_{l}") for l in range(4)]
        s_pe1 = sem("small_product_ready")
        s_mm = sem("stage1_operand_ready")
        s_z = sem("z_tile_ready")
        s_zc = sem("z_tile_copied")
        s_kexp = sem("key_exponentials_ready")
        s_kneg = sem("key_maximum_ready")
        s_qsub = sem("query_shifted")
        s_qexp = sem("query_exponentials_ready")
        s_mix = sem("mix_tile_ready")
        s_mixa = sem("mix_tile_added")
        s_bound = sem("window_bounds_ready")
        s_ohr = sem("one_hot_sources_ready")
        s_odr = sem("weighted_destinations_ready")
        s_ohf = sem("one_hot_buffer_free")
        s_win = sem("window_summed")
        s_wevac = sem("window_banks_free")
        s_stg = sem("window_staged")
        s_stf = sem("window_stage_free")
        s_agg = sem("aggregate_ready")
        s_agga = sem("aggregate_added")
        s_moew = sem("expert_constants_loaded")
        s_ew = [sem(f"expert_weights_loaded_{k}") for k in range(2)]
        s_lg = sem("router_product_ready")
        s_ro = sem("router_operand_ready")
        s_pm = sem("router_maximum_ready")
        s_pexp = sem("router_exponentials_ready")
        s_jc = sem("search_constants_built")
        s_es = sem("same_expert_mask_ready")
        s_esc = sem("same_expert_mask_copied")
        s_ok = sem("search_counts_ready")
        s_oks = sem("search_counts_summed")
        s_h = sem("hidden_product_ready")
        s_gelu = sem("hidden_ready")
        s_oy = sem("expert_product_ready")
        s_oa = sem("expert_product_added")
        s_w1 = sem("layer1_weights_loaded")
        s_bc = sem("rows_broadcast")
        s_bcc = sem("row_broadcasts_copied")
        s_y = sem("y_tile_ready")
        s_yc = sem("y_tile_copied")
        s_dsum = sem("degree_partial_ready")
        s_deg = sem("degree_ready")
        s_agg1 = sem("mean_aggregate_ready")
        s_agga1 = sem("mean_aggregate_added")
        s_q1 = sem("query_tile_ready")
        s_q1s = sem("query_tile_shifted")
        s_q1e = sem("query_tile_exponentials")
        s_q1n = sem("query_tile_normalised")
        s_k1 = sem("key_block_ready")
        s_k1m = sem("key_block_maximum")
        s_k1e = sem("key_block_exponentials")
        s_v1 = sem("value_tile_ready")
        s_v1c = sem("value_tile_copied")
        s_kr = sem("key_rows_ready")
        s_krc = sem("key_rows_copied")
        s_cx = sem("context_ready")
        s_cxc = sem("context_masked")
        s_m1 = sem("output_matrix_ready")
        s_m1c = sem("output_matrix_scaled")
        s_qt = sem("query_transposed")
        s_qtc = sem("query_transpose_copied")
        s_mo = sem("mixer_output_ready")
        s_moc = sem("mixer_output_copied")
        s_var1 = sem("mixer_variance_ready")
        s_sd1 = sem("mixer_deviation_ready")
        s_w4 = sem("product_key_weights_loaded")
        s_q4 = sem("head_query_ready")
        s_q4c = sem("head_query_copied")
        s_sc4 = sem("head_scores_ready")
        s_scf = sem("head_scores_free")
        s_rows = sem("row_numbers_ready")
        s_sub4 = sem("scores_shifted")
        s_exp4 = sem("score_exponentials_ready")
        s_gat = [sem(f"slot_{k}_gathered") for k in range(SLOTS)]
        s_slot = sem("slot_free")
        s_passed = [sem(f"waits_passed_{k}") for k in range(2)]
        s_vals = sem("head_values_ready")
        s_dg = sem("diagonal_ready")
        s_xo = sem("tile_output_added")
        s_st = sem("tile_stored")
        block = ctx.enter_context(nc.Block())

        def stage_barrier(engine, k):
            engine.drain().then_inc(stage_end[k], 1)
            engine.wait_ge(stage_end[k], 5)

        def window_bounds(engine, w):
            word = engine.value_load(bounds[0:1, ds(w, 1)], min_val=0, max_val=(1 << 30) - 1)
            first = word & ((1 << FIRST_BITS) - 1)
            turns = (word // (1 << FIRST_BITS)) & ((1 << TURN_BITS) - 1)
            begin = engine.snap(word // (1 << (FIRST_BITS + TURN_BITS)) * OHB).with_bounds(max_val=NBE * NW - OHB)
            end = engine.snap(begin + turns * OHB).with_bounds(max_val=NBE * NW)
            lower = engine.snap(begin - first) if engine is not nc.tensor else None
            return begin, end, lower

        def edge_block(place, lower):
            return (place - lower).with_bounds(min_val=0, max_val=NBE - 1)

        def store(sp):
            s_out = sem("out_stored")
            sp.dma_start(out[0:(T - 1) * P, :].rearrange("(t p) n -> p t n", p=P),
                         X[:, 0:(T - 1) * D].rearrange("p (t n) -> p t n", n=D)).then_inc(s_out, 16)
            sp.dma_start(out[(T - 1) * P:N, :], X[0:TAIL, (T - 1) * D:T * D]).then_inc(s_out, 16)
            sp.wait_ge(s_out, 32)

        @block.sync
        def _(sp):
            xv = d["x"].rearrange("(t p) n -> p t n", p=P)
            sp.dma_start(raw_dst, d["dst"]).then_inc(s_edges, 16)
            sp.dma_start(raw_src, d["src"]).then_inc(s_edges, 16)
            sp.dma_start(raw_w, d["edge_weight"]).then_inc(s_edges, 16)
            sp.dma_start(X[:, :].rearrange("p (t n) -> p t n", t=T), xv).then_inc(s_x, 16)
            for dst, name in ((W0, "L0_gnn_W"), (Win, "L0_mix_W_in"), (WinT, "L0_mix_W_in_T"), (Wout, "L0_mix_W_out")):
                sp.dma_start(dst.rearrange("p (i n) -> p i n", i=KD),
                             d[name].rearrange("(i p) n -> p i n", p=P)).then_inc(s_w0, 16)
            sp.wait_ge(s_const, 1)
            for h2 in range(2):
                rows = slice(64 * h2, 64 * h2 + 64)
                sp.dma_start(bdqk[rows, 4 * h2:4 * h2 + 4], d["L0_mix_W_q"]).then_inc(s_w0, 16)
                sp.dma_start(bdqk[rows, 8 + 4 * h2:12 + 4 * h2], d["L0_mix_W_k"]).then_inc(s_w0, 16)
                sp.dma_start(bdv[rows, rows], d["L0_mix_W_v_T"]).then_inc(s_w0, 16)
            sp.dma_start(binc, d["L0_mix_b_in_col"]).then_inc(s_w0, 16)
            sp.dma_start(binr, d["L0_mix_b_in"].unsqueeze(0)).then_inc(s_w0, 16)
            sp.dma_start(boutr, d["L0_mix_b_out"].unsqueeze(0)).then_inc(s_w0, 16)
            stage_barrier(sp, 0)
            for dst, name in ((wr, "L0_ffn_Wr"), (b2, "L0_ffn_b2")):
                sp.dma_start(dst, d[name]).then_inc(s_moew, 16)
            w1v = d["L0_ffn_W1"].rearrange("e (i p) n -> p e i n", p=P)
            w2v = d["L0_ffn_W2"].rearrange("e (f p) n -> p e f n", p=P)

            b1v = d["L0_ffn_b1_col"].rearrange("p (e f) -> p e f", e=NE)

            def expert_weights(e, k):
                w = EW[k]
                sp.dma_start(w[:, 0:1024].rearrange("p (e i n) -> p e i n", e=1, i=KD), w1v[:, ds(e, 1)]).then_inc(s_ew[k], 16)
                sp.dma_start(w[:, 1024:2048].rearrange("p (e f n) -> p e f n", e=1, f=FB), w2v[:, ds(e, 1)]).then_inc(s_ew[k], 16)
                sp.dma_start(b1k[k].rearrange("p (e f) -> p e f", e=1), b1v[:, ds(e, 1)]).then_inc(s_ew[k], 16)

            for e in range(2):
                expert_weights(e, e)
            stage_barrier(sp, 1)
            if last_stage == 1:
                return store(sp)
            with sp.Fori(1, NE // 2) as pair:
                for k in range(2):
                    e = pair * 2 + k
                    sp.wait_ge(s_oy, e * T + 1)
                    expert_weights(e, k)
            stage_barrier(sp, 2)
            if last_stage == 2:
                return store(sp)
            for dst, name in ((Wg1, "L1_gnn_W_T"), (Wqkv, "L1_mix_w_qkv_T"), (Wo1, "L1_mix_w_out_T")):
                sp.dma_start(dst.rearrange("p (i n) -> p i n", i=KD),
                             d[name].rearrange("(i p) n -> p i n", p=P)).then_inc(s_w1, 16)
            for dst, name in ((gamr, "L1_mix_gamma"), (br1, "L1_gnn_b"), (alr, "L1_gnn_alpha")):
                sp.dma_start(dst, d[name].unsqueeze(0)).then_inc(s_w1, 16)
            stage_barrier(sp, 3)
            if last_stage == 3:
                return store(sp)
            sp.dma_start(Wq4.rearrange("p (i n) -> p i n", i=KD),
                         d["L1_ffn_Wq"].rearrange("(i p) n -> p i n", p=P)).then_inc(s_w4, 16)
            sp.dma_start(keysT.rearrange("p (h n) -> p h n", h=PH),
                         d["L1_ffn_keys_T"].rearrange("h p n -> p h n")).then_inc(s_w4, 16)
            sp.dma_start(bq4, d["L1_ffn_bq_col"]).then_inc(s_w4, 16)
            with sp.Fori(0, T - 1) as t:
                sp.wait_ge(s_xo, t + 1)
                sp.dma_start(out[ds(t * P, P), :], X[:, ds(t * D, D)]).then_inc(s_st, 16)
            sp.wait_ge(s_xo, T)
            sp.dma_start(out[(T - 1) * P:N, :], X[0:TAIL, (T - 1) * D:T * D]).then_inc(s_st, 16)
            sp.wait_ge(s_st, 16 * T)

        @block.gpsimd
        def _(pool):
            built = Chain(pool, s_const)
            built(pool.memset(A0[:, q0:q0 + 1012], 0.0))
            built(pool.memset(ident[:, :], 0.0))
            built(pool.memset(ones[:, :], 1.0))
            built(pool.memset(headmask, 1.0))
            built(pool.memset(epsc, EPS))
            built(pool.affine_select(out=ident[:, :], in_=ident[:, :], compare_op=ALU.not_equal, fill=1.0,
                                     base=0, pattern=[[-1, P]], channel_multiplier=1))
            built(pool.iota(iota16[:, :], [[1, NP]], base=0, channel_multiplier=0))
            built(pool.iota(winlo, [[0, 1]], base=0, channel_multiplier=WIN, allow_small_or_imprecise_dtypes=True))
            built(pool.iota(winhi, [[0, 1]], base=WIN - 1, channel_multiplier=WIN, allow_small_or_imprecise_dtypes=True))
            built(pool.iota(bup, [[1, NBP]], base=1, channel_multiplier=0, allow_small_or_imprecise_dtypes=True))
            built(pool.iota(bdown, [[-1, NBP]], base=NB, channel_multiplier=0, allow_small_or_imprecise_dtypes=True))
            built(pool.iota(bthird, [[OHB, NBP]], base=0, channel_multiplier=0, allow_small_or_imprecise_dtypes=True))
            built(pool.iota(windows[:, :], [[1, NW]], base=0, channel_multiplier=0, allow_small_or_imprecise_dtypes=True))
            built(pool.iota(iota32[:, :], [[1, WIN]], base=0, channel_multiplier=0, allow_small_or_imprecise_dtypes=True))
            built(pool.memset(tri, 1.0))
            built(pool.affine_select(out=tri, in_=tri, compare_op=ALU.is_gt, fill=0.0,
                                     base=0, pattern=[[1, NW]], channel_multiplier=-1))
            hm = headmask.rearrange("p (h c) -> p h c", h=HEADS)
            built(pool.affine_select(out=hm, in_=hm, compare_op=ALU.is_ge, fill=0.0,
                                     base=0, pattern=[[-KR, HEADS], [0, 64]], channel_multiplier=1))
            built(pool.affine_select(out=hm, in_=hm, compare_op=ALU.is_ge, fill=0.0,
                                     base=KR - 1, pattern=[[KR, HEADS], [0, 64]], channel_multiplier=-1))
            assert built.n == CONSTANTS
            stage_barrier(pool, 0)
            A0v = A0.rearrange("p (s n) -> p s n", s=T)

            def destinations(w):
                begin, end, lower = window_bounds(pool, w)
                with pool.Fori(begin, end, OHB) as place:
                    for k in range(OHB):
                        b = edge_block(place + k, lower)
                        pool.wait_ge(s_ohf, place + (k + 1))
                        pool.tensor_tensor(ohd[k].rearrange("p (q c) -> p q c", q=4),
                                           eq32[:, ds(b * WIN, WIN)].unsqueeze(1).to_broadcast([P, 4, WIN]),
                                           wparts[:, ds(b * 4, 4)].unsqueeze(2).to_broadcast([P, 4, WIN]),
                                           ALU.mult).then_inc(s_odr, 1)

            def add_parts(w, k):
                st = staged[:, 960 * k:960 * k + 960].rearrange("p (s q c) -> p s q c", s=T, q=3)
                tmp = summed[:, 320 * k:320 * k + 320].rearrange("p (s c) -> p s c", s=T)
                pool.wait_ge(s_stg, w + 1)
                pool.tensor_tensor(tmp, st[:, :, 0, :], st[:, :, 1, :], ALU.add).then_inc(s_po, 1)
                pool.wait_ge(s_po, w + 1)
                pool.tensor_tensor(A0v[:, :, ds(w * WIN, WIN)], tmp, st[:, :, 2, :], ALU.add).then_inc(s_stf, 1)

            destinations(0)
            with pool.Fori(0, NW // 2 - 1) as pair:
                for k in range(2):
                    destinations(pair * 2 + (k + 1))
                    add_parts(pair * 2 + k, k)
            destinations(NW - 1)
            add_parts(NW - 2, 0)
            add_parts(NW - 1, 1)
            stage_barrier(pool, 1)
            if last_stage == 1:
                return
            jb = Chain(pool, s_jc)
            jb(pool.iota(jcol, [[0, 1]], base=0, channel_multiplier=1))
            jb(pool.memset(erep, 1.0))
            er = erep.rearrange("p (j e) -> p j e", e=NE)
            jb(pool.affine_select(out=er, in_=er, compare_op=ALU.is_equal, fill=0.0,
                                  base=0, pattern=[[0, P // NE], [-1, NE]], channel_multiplier=1))
            assert jb.n == 3
            with pool.Fori(0, T) as s:
                pool.tensor_copy(A0[:, ds(s * NP, NP)], A1C[:, ds(s * NP, NP)])
            stage_barrier(pool, 2)
            if last_stage == 2:
                return
            masks = Chain(pool, s_po2)
            masks(pool.memset(bmask, 0.0))
            for h2 in range(2):
                masks(pool.memset(bmask[64 * h2:64 * h2 + 64, 64 * h2:64 * h2 + 64], 1.0))
            masks(pool.iota(iota8, [[1, TK]], base=0, channel_multiplier=0, allow_small_or_imprecise_dtypes=True))
            stage_barrier(pool, 3)
            if last_stage == 3:
                return
            with pool.Fori(0, T // 2) as pair:
                for k in range(2):
                    t = pair * 2 + k
                    pool.wait_ge(s_rows, t + 1)
                    for g in range(GPT):
                        if g % 4 == 0:
                            pool.wait_ge(s_slot, t * GPT + (g + 4))
                            pool.sem_inc(s_passed[0], 1)
                        pool.indirect_dma_start(slot[g % SLOTS], None, d["L1_ffn_w"],
                                                bass.IndirectOffsetOnAxis(ap=rowid[k][:, g:g + 1], axis=0)
                                                ).then_inc(s_gat[g % SLOTS], 16)
            pool.drain()

        @block.scalar
        def _(act):
            link = Chain(act, s_sc)

            def deviation(l, eps=epsc):
                act.wait_ge(s_var[l], 1)
                var = mv.rearrange("p (t c) -> p t c", c=2)[:, :, 1]
                act.activation(rstd2, var, ACT.Sqrt, bias=eps).then_inc(s_sd[l], 1)

            def transpose_copies(l):
                with act.Fori(0, T // 2) as pair:
                    for k in range(2):
                        act.wait_ge(s_xtp[l], pair * 2 + (k + 1))
                        act.activation(XNT3[:, :, ds((pair * 2 + k) * P, P)],
                                       bank(k).rearrange("p (i c) -> p i c", i=KD), ACT.Copy).then_inc(s_xt[l], 1)

            act.wait_ge(s_const, CONSTANTS)
            deviation(0)
            transpose_copies(0)
            act.wait_ge(s_pe1, 5)
            act.activation(WF, bank(5, 256), ACT.Copy).then_inc(s_mm, 1)
            act.activation(qkb, bank(6, 64, 1), ACT.Copy).then_inc(s_mm, 1)
            for j in range(KD):
                act.wait_ge(s_pe1, 6 + j)
                act.activation(VO[:, 512 * j:512 * j + 512], bank(j), ACT.Copy).then_inc(s_mm, 1)
            with act.Fori(0, T // 2) as pair:
                for k in range(2):
                    act.wait_ge(s_z, pair * 2 + (k + 1))
                    act.activation(ZF[:, ds((pair * 2 + k) * D, D)], bank(k), ACT.Copy).then_inc(s_zc, 1)
            act.wait_ge(s_qsub, 1)
            act.activation(qrow, qrow, ACT.Exp).then_inc(s_qexp, 1)
            act.wait_ge(s_kneg, 1)
            act.activation(kTe[:, 0:N], PS[0:HR, 1024:1024 + N], ACT.Exp, bias=kneg, accum_out=ksum).then_inc(s_kexp, 1)
            stage_barrier(act, 0)
            A1v = A1C.rearrange("p (s n) -> p s n", s=T)
            with act.Fori(0, NW // 2) as pair:
                for k in range(2):
                    w = pair * 2 + k
                    banks = PS[:, 1536 * k:1536 * k + NP].rearrange("p (s c) -> p s c", s=T)
                    act.wait_ge(s_win, w + 1)
                    act.wait_ge(s_stf, w + 1)
                    act.activation(staged[:, 960 * k:960 * k + 960].rearrange("p (s c) -> p s c", s=T),
                                   banks[:, :, 0:96], ACT.Copy).then_inc(s_stg, 1)
                    act.activation(A1v[:, :, ds(w * WIN, WIN)], banks[:, :, 96:128], ACT.Copy).then_inc(s_wevac, 1)
            stage_barrier(act, 1)
            if last_stage == 1:
                return
            deviation(1)
            transpose_copies(1)
            act.wait_ge(s_pm, 1)
            act.activation(prob[:, 0:N], PS[0:NE, 1024:1024 + N], ACT.Exp, bias=pneg, accum_out=psumc).then_inc(s_pexp, 1)
            act.wait_ge(s_lg, 2)
            act.activation(probR, PS[:, 1024:1024 + NP], ACT.Copy).then_inc(s_pexp, 1)
            act.wait_ge(s_es, 1)
            act.activation(esame, bank(6, P), ACT.Copy).then_inc(s_esc, 1)
            act.wait_ge(s_moew, 32)
            with act.Fori(0, NE // 2) as pair:
                for k in range(2):
                    e = pair * 2 + k
                    act.wait_ge(s_oy, e * T + 1)
                    for u, (f, (c0, cn)) in enumerate([(f, c) for f in range(FB) for c in CHUNKS]):
                        act.wait_ge(s_h, e * 6 + (u + 1))
                        act.activation(hT[k][:, f * NP + c0:f * NP + c0 + cn], bank(u % 3, cn), ACT.Gelu,
                                       bias=b1k[k][:, f:f + 1]).then_inc(s_gelu, 1)
            stage_barrier(act, 2)
            if last_stage == 2:
                return
            deviation(2)
            transpose_copies(2)
            with act.Fori(0, T // 2) as pair:
                for k in range(2):
                    act.wait_ge(s_y, pair * 2 + (k + 1))
                    act.activation(ZF[:, ds((pair * 2 + k) * D, D)], bank(k), ACT.Copy).then_inc(s_yc, 1)
            with act.Fori(0, T) as t:
                act.wait_ge(s_q1s, t + 1)
                act.activation(QR[:, ds(t * D, D)], QR[:, ds(t * D, D)], ACT.Exp).then_inc(s_q1e, 1)
            for j in range(KD):
                act.wait_ge(s_k1m, j + 1)
                act.activation(kT1[:, NP * j:NP * j + N], PS[:, 1536 * (j % 2):1536 * (j % 2) + N], ACT.Exp,
                               bias=kneg1[:, j:j + 1], accum_out=ksum1[:, j:j + 1]).then_inc(s_k1e, 1)
            with act.Fori(0, T // 2) as pair:
                for k in range(2):
                    act.wait_ge(s_v1, pair * 2 + (k + 1))
                    act.activation(V1[:, ds((pair * 2 + k) * D, D)], bank(6 + k), ACT.Copy).then_inc(s_v1c, 1)
            with act.Fori(0, T // 2) as pair:
                for k in range(2):
                    act.wait_ge(s_kr, pair * 2 + (k + 1))
                    act.activation(kR1[:, ds((pair * 2 + k) * D, D)], bank(k), ACT.Copy).then_inc(s_krc, 1)
            qT3 = qT1.rearrange("p (j n) -> p j n", j=KD)
            with act.Fori(0, T // 2) as pair:
                for k in range(2):
                    act.wait_ge(s_qt, pair * 2 + (k + 1))
                    act.activation(qT3[:, :, ds((pair * 2 + k) * P, P)],
                                   bank(k).rearrange("p (j c) -> p j c", j=KD), ACT.Copy).then_inc(s_qtc, 1)
            with act.Fori(0, T // 2) as pair:
                for k in range(2):
                    act.wait_ge(s_mo, pair * 2 + (k + 1))
                    act.activation(MO[:, ds((pair * 2 + k) * D, D)], bank(6 + k), ACT.Copy).then_inc(s_moc, 1)
            act.wait_ge(s_var1, 1)
            act.activation(rstd2, mv.rearrange("p (t c) -> p t c", c=2)[:, :, 1], ACT.Sqrt, bias=epsc).then_inc(s_sd1, 1)
            stage_barrier(act, 3)
            if last_stage == 3:
                return
            deviation(3)
            transpose_copies(3)
            act.wait_ge(s_w4, 48)

            def head_queries(t):
                for h in range(PH):
                    if h % 4 == 0:
                        act.wait_ge(s_q4, t * 2 + (h // 4 + 1))
                    act.activation(qT4[:, P * h:P * h + P], bank(h // 4, P, start=P * (h % 4)), ACT.Identity,
                                   bias=bq4[:, h:h + 1]).then_inc(s_q4c, 1)

            def score_exponentials(t, k):
                act.wait_ge(s_sub4, t + 1)
                act.activation(soft[k], soft[k], ACT.Exp).then_inc(s_exp4, 1)

            def up_diagonals(t, k, more):
                if more:
                    head_queries(t + 1)
                for h in range(PH):
                    if more and h == 6:
                        score_exponentials(t + 1, 1 - k)
                    act.wait_ge(s_vals, t * PH + (h + 1))
                    for g in range(TK * h, TK * h + TK):
                        act.wait_ge(s_slot, t * GPT + (g + 1 + SLOTS - 4))
                        act.activation(diag[g % 4], ident[:, :], ACT.Copy, scale=vals[:, g:g + 1]).then_inc(s_dg, 1)

            head_queries(0)
            score_exponentials(0, 0)
            with act.Fori(0, T // 2 - 1) as pair:
                for k in range(2):
                    up_diagonals(pair * 2 + k, k, True)
            up_diagonals(T - 2, 0, True)
            up_diagonals(T - 1, 1, False)
            act.drain()

        @block.vector
        def _(v):
            link = Chain(v, s_dv)

            def statistics(src, l, ready=None):
                with v.Fori(0, T) as t:
                    if ready is not None:
                        v.wait_ge(ready, t + 1)
                    link.enter(t, 1)
                    link(v.bn_stats(stat[:, ds(t * 6, 6)], src[:, ds(t * D, D)]))
                link.leave(T)
                for t in range(T):
                    last = v.bn_aggr(mv[:, 2 * t:2 * t + 2], stat[:, 6 * t:6 * t + 6])
                last.then_inc(s_var[l], 1)
                v.wait_ge(s_sd[l], 1)
                link(v.reciprocal(rstd, rstd2))

            def normalise(l):
                with v.Fori(0, T) as t:
                    v.tensor_scalar(XN[:, ds(t * D, D)], X[:, ds(t * D, D)], mv[:, ds(t * 2, 1)], rstd[:, ds(t, 1)],
                                    ALU.subtract, ALU.mult).then_inc(s_xn[l], 1)

            v.wait_ge(s_edges, 48)
            link(v.tensor_copy(dstf, raw_dst))
            v.tensor_copy(srcf, raw_src).then_inc(s_mm, 1)
            link(v.tensor_scalar(dtmp, raw_dst, WIN - 1, None, ALU.bitwise_and))
            link(v.tensor_copy(dlow, dtmp))
            wp = wparts[:, :].rearrange("p (b q) -> p b q", q=4)
            link(v.tensor_copy(wp[:, :, 0], raw_w))
            link(v.tensor_tensor(res1, raw_w, wp[:, :, 0], ALU.subtract))
            link(v.tensor_copy(wp[:, :, 1], res1))
            link(v.tensor_tensor(res1, res1, wp[:, :, 1], ALU.subtract))
            v.tensor_copy(wp[:, :, 2], res1)
            v.memset(wp[:, :, 3], 1.0)
            v.wait_ge(s_const, CONSTANTS)
            v.wait_ge(s_pe1, 1)
            dT = bank(0, 384).rearrange("p (c e) -> p c e", c=3)
            link(v.tensor_reduce(blkmin, dT, AX.X, ALU.min))
            link(v.tensor_reduce(blkmax, dT, AX.X, ALU.max))
            for c in range(3):
                v.tensor_scalar(dmin[:, P * c:P * c + P], ident[:, :], blkmin[:, c:c + 1], None, ALU.mult)
                last = v.tensor_scalar(dmax[:, P * c:P * c + P], ident[:, :], blkmax[:, c:c + 1], None, ALU.mult)
            last.then_inc(s_mm, 1)
            v.wait_ge(s_pe1, 2)
            hb, bb = hit[:, 0:NB], hitb[:, 0:NB]
            link(v.tensor_scalar(hb, bank(1, NB, NW), winhi, None, ALU.is_le))
            link(v.scalar_tensor_tensor(hb, bank(2, NB, NW), winlo, hb, ALU.is_ge, ALU.mult))
            link(v.tensor_tensor(bb, hb, bup[:, 0:NB], ALU.mult))
            link(v.tensor_reduce(wend, bb, AX.X, ALU.max))
            link(v.tensor_tensor(bb, hb, bdown[:, 0:NB], ALU.mult))
            link(v.tensor_reduce(wfirst, bb, AX.X, ALU.max))
            link(v.tensor_scalar(wfirst, wfirst, -1.0, float(NB), ALU.mult, ALU.add))
            link(v.tensor_scalar(wfirst, wfirst, float(NB - 1), None, ALU.min))
            link(v.scalar_tensor_tensor(wend, wfirst, 1.0, wend, ALU.add, ALU.max))
            link(v.tensor_tensor(wend, wend, wfirst, ALU.subtract))
            v.tensor_scalar(bb[:, 0:TURNS], bthird[:, 0:TURNS], wend, None, ALU.is_lt, ALU.add,
                            accum_out=wcnt).then_inc(s_mm, 1)
            v.wait_ge(s_pe1, 3)
            link(v.tensor_copy(woff, bank(3, 1, NW)))
            for c, col in enumerate((wfirst, wcnt, woff)):
                last = v.tensor_scalar(flat3[:, NW * c:NW * c + NW], ident[0:NW, 0:NW], col, None, ALU.mult)
            last.then_inc(s_mm, 1)
            v.wait_ge(s_pe1, 4)
            link(v.tensor_copy(bounds3, bank(4, 3 * NW, 1)))
            link(v.tensor_scalar(bounds3[:, NW:2 * NW], bounds3[:, NW:2 * NW], FIRST_BITS, None, ALU.logical_shift_left))
            link(v.tensor_scalar(bounds3[:, 2 * NW:], bounds3[:, 2 * NW:], FIRST_BITS + TURN_BITS, None,
                                 ALU.logical_shift_left))
            link(v.tensor_tensor(bounds, bounds3[:, 0:NW], bounds3[:, NW:2 * NW], ALU.bitwise_or))
            v.tensor_tensor(bounds, bounds, bounds3[:, 2 * NW:], ALU.bitwise_or).then_inc(s_bound, 1)
            v.wait_ge(s_x, 16)
            statistics(X, 0)
            normalise(0)
            qv = qrow.rearrange("p (a r) -> p a r", r=KR)
            qb = qmax.unsqueeze(2).to_broadcast([P, T * HEADS, KR])
            v.wait_ge(s_pe1, 10)
            link(v.tensor_reduce(qmax, bank(6, 320).rearrange("p (a r) -> p a r", r=KR), AX.X, ALU.max))
            v.tensor_tensor(qv, bank(6, 320).rearrange("p (a r) -> p a r", r=KR), qb, ALU.subtract).then_inc(s_qsub, 1)
            v.wait_ge(s_pe1, 11)
            v.tensor_reduce(kneg, PS[0:HR, 1024:1024 + N], AX.X, ALU.max, negate=True).then_inc(s_kneg, 1)
            v.memset(kTe[:, N:NP], 0.0).then_inc(s_mm, 1)
            v.wait_ge(s_qexp, 1)
            link(v.tensor_reduce(qmax, qv, AX.X, ALU.add))
            link(v.reciprocal(qmax, qmax))
            v.tensor_tensor(qv, qv, qb, ALU.mult).then_inc(s_mm, 1)
            v.wait_ge(s_kexp, 1)
            link(v.reciprocal(ksum, ksum))
            v.wait_ge(s_pe1, 12)
            v.tensor_copy(qTs, PS[0:HR, 1024:1024 + NP]).then_inc(s_mm, 1)
            v.wait_ge(s_pe1, 13)
            v.tensor_copy(krow, bank(6, 320)).then_inc(s_mm, 1)
            v.wait_ge(s_pe1, 14)
            v.tensor_copy(kxT, bank(7, 128)).then_inc(s_mm, 1)
            v.wait_ge(s_pe1, 15)
            link(v.tensor_scalar(kxm, bank(5, 512, HR), ksum, None, ALU.mult))
            v.wait_ge(s_pe1, 16)
            link(v.tensor_tensor(kxm, kxm, bank(4, 512, HR), ALU.add))
            v.tensor_tensor(kxm, kxm, headmask, ALU.mult).then_inc(s_mm, 1)
            v.wait_ge(s_pe1, 17)
            v.tensor_copy(kxmT, bank(7, 128)).then_inc(s_mm, 1)
            v.wait_ge(s_pe1, 18)
            v.tensor_copy(Mx, bank(5, 512, HR)).then_inc(s_mm, 1)
            with v.Fori(0, T // 2) as pair:
                for k in range(2):
                    t = pair * 2 + k
                    v.wait_ge(s_mix, t + 1)
                    v.tensor_tensor(X[:, ds(t * D, D)], bank(k), X[:, ds(t * D, D)], ALU.add).then_inc(s_mixa, 1)
            link(v.tensor_tensor(eq32.rearrange("p (b c) -> p b c", c=WIN),
                                 iota32[:, :].unsqueeze(1).to_broadcast([P, NBV, WIN]),
                                 dlow[:, 0:NBV].unsqueeze(2).to_broadcast([P, NBV, WIN]), ALU.is_equal))
            link(v.tensor_scalar(dtmp, raw_dst, 5, None, ALU.arith_shift_right))
            v.tensor_copy(dwin, dtmp)
            stage_barrier(v, 0)
            v.memset(zero_b, 0.0).then_inc(s_ohr, 1)
            iw = iota16[:, :]
            v.wait_ge(s_ohr, 1)
            with v.Fori(0, NW) as w:
                begin, end, lower = window_bounds(v, w)
                v.wait_ge(s_ohr, begin + 1)
                link.enter(w, 1)
                link(v.tensor_scalar(inwin, dwin[:, 0:NBV], windows[:, ds(w, 1)], None, ALU.is_equal))
                v.sem_inc(s_passed[1], 1)
                with v.Fori(begin, end, OHB) as place:
                    for k in range(OHB):
                        b = edge_block(place + k, lower)
                        v.wait_ge(s_ohf, place + (k + 1))
                        v.tensor_scalar(ohs[k], iw, srcf[:, ds(b, 1)], inwin[:, ds(b, 1)],
                                        ALU.is_equal, ALU.mult).then_inc(s_ohr, 1)
            link.leave(NW)
            with v.Fori(0, T // 2) as pair:
                for k in range(2):
                    t = pair * 2 + k
                    v.wait_ge(s_agg, t + 1)
                    v.scalar_tensor_tensor(X[:, ds(t * D, D)], bank(6 + k), 0.0, X[:, ds(t * D, D)],
                                           ALU.max, ALU.add).then_inc(s_agga, 1)
            stage_barrier(v, 1)
            if last_stage == 1:
                return
            statistics(X, 1)
            normalise(1)
            v.wait_ge(s_jc, 3)
            link(v.tensor_scalar(jcl, jcol, 3, None, ALU.arith_shift_right))
            link(v.tensor_scalar(jbits[:, 0:1], jcl, 4.0, None, ALU.min))
            link(v.tensor_scalar(jbits[:, 0:1], jbits[:, 0:1], 28, None, ALU.logical_shift_left))
            for r in range(1, ROUNDS):
                link(v.tensor_scalar(jbits[:, r:r + 1], jcl, 28 - 4 * r, None, ALU.logical_shift_left))
            for r in range(ROUNDS):
                link(v.memset(scale2[:, r:r + 1], float(1 << (28 - 4 * r))))
            link(v.memset(basei, 0))
            v.wait_ge(s_lg, 1)
            v.tensor_reduce(pneg, PS[0:NE, 1024:1024 + N], AX.X, ALU.max, negate=True).then_inc(s_pm, 1)
            v.wait_ge(s_pexp, 1)
            link(v.reciprocal(psumc, psumc))
            link(v.memset(prob[:, N:NP], 0.0))
            v.tensor_scalar(prob[:, 0:N], prob[:, 0:N], psumc, None, ALU.mult).then_inc(s_ro, 1)
            v.wait_ge(s_pexp, 2)
            with v.Fori(0, ROUNDS) as r:
                link.enter(r, 5)
                link(v.tensor_tensor(thri, basei, jbits[:, ds(r, 1)], ALU.bitwise_or))
                link(v.tensor_scalar(sel1[:, 0:N], probR[:, 0:N], thrf, None, ALU.is_ge, ALU.add, accum_out=cntc))
                v.tensor_scalar(okc, cntc, float(CAP), None, ALU.is_ge).then_inc(s_ok, 1)
                v.wait_ge(s_oks, r + 1)
                link(v.tensor_scalar(stepf, bank(5, 1), -1.0, scale2[:, ds(r, 1)], ALU.add, ALU.mult))
                link(v.tensor_copy(stepi, stepf))
                link(v.tensor_tensor(basei, basei, stepi, ALU.bitwise_or))
            link.leave(ROUNDS)
            thr8 = basei[0:NE, :].bitcast(F32)
            g8, e8, c8 = sel1[0:NE, 0:N], sel2[0:NE, 0:N], probR[0:NE, 0:N]
            link(v.tensor_scalar(g8, prob[:, 0:N], thr8, None, ALU.is_gt, ALU.add, accum_out=cgt))
            link(v.tensor_scalar(e8, prob[:, 0:N], thr8, None, ALU.is_equal))
            link(v.tensor_tensor_scan(c8, e8, e8, 0.0, ALU.add, ALU.max))
            link(v.tensor_scalar(need, cgt, -1.0, float(CAP), ALU.mult, ALU.add))
            link(v.scalar_tensor_tensor(e8, c8, need, e8, ALU.is_le, ALU.mult))
            link(v.tensor_tensor(g8, g8, e8, ALU.add))
            v.tensor_tensor(prob[:, 0:N], prob[:, 0:N], g8, ALU.mult).then_inc(s_ro, 1)
            v.wait_ge(s_lg, 3)
            link(v.tensor_copy(gate, bank(2, NE * T)))
            v.sem_inc(s_ro, 1)
            for t in range(T):
                v.wait_ge(s_oy, t + 2)
                v.tensor_tensor(X[:, D * t:D * t + D], bank(3 + t % 5), X[:, D * t:D * t + D], ALU.add).then_inc(s_oa, 1)
            with v.Fori(0, NE) as e:
                for t in range(T):
                    v.wait_ge(s_oy, e * T + (T + t + 2))
                    v.scalar_tensor_tensor(X[:, D * t:D * t + D], bank(3 + t % 5), gate[:, ds(e + NE * t, 1)],
                                           X[:, D * t:D * t + D], ALU.mult, ALU.add).then_inc(s_oa, 1)
            stage_barrier(v, 2)
            if last_stage == 2:
                return
            statistics(X, 2)
            normalise(2)
            v.wait_ge(s_xn[2], T)
            v.wait_ge(s_bc, 1)
            link(v.tensor_copy(gam, bank(7)))
            link(v.tensor_copy(alphac, bank(5, 1)))
            link(v.tensor_scalar(ab, bank(6), alphac, None, ALU.mult))
            v.sem_inc(s_bcc, 1)
            v.tensor_reduce(a1sum, A0.rearrange("p (s n) -> p n s", s=T), AX.X, ALU.add).then_inc(s_dsum, 1)
            with v.Fori(0, T) as t:
                xt = X[:, ds(t * D, D)]
                link.enter(t, 2)
                link(v.tensor_tensor(xt, xt, XN[:, ds(t * D, D)], ALU.add))
                link(v.tensor_tensor(xt, xt, ab, ALU.add))
            link.leave(T)
            v.wait_ge(s_deg, 1)
            link(v.tensor_scalar(degc, bank(4, T), 1.0, None, ALU.max))
            link(v.reciprocal(degc, degc))
            link(v.tensor_scalar(adeg, degc, alphac, None, ALU.mult))
            with v.Fori(0, T // 2) as pair:
                for k in range(2):
                    t = pair * 2 + k
                    v.wait_ge(s_agg1, t + 1)
                    v.scalar_tensor_tensor(X[:, ds(t * D, D)], bank(2 + k), adeg[:, ds(t, 1)], X[:, ds(t * D, D)],
                                           ALU.mult, ALU.add).then_inc(s_agga1, 1)
            with v.Fori(0, T // 2) as pair:
                link.enter(pair, 2)
                for k in range(2):
                    t = pair * 2 + k
                    qm = qm1[:, HEADS * k:HEADS * k + HEADS]
                    v.wait_ge(s_q1, t + 1)
                    qp = bank(6 + k).rearrange("p (h c) -> p h c", h=HEADS)
                    link(v.tensor_reduce(qm, qp, AX.X, ALU.max))
                    v.tensor_tensor(QR[:, ds(t * D, D)].rearrange("p (h c) -> p h c", h=HEADS), qp,
                                    qm.unsqueeze(2).to_broadcast([P, HEADS, 64]), ALU.subtract).then_inc(s_q1s, 1)
            link.leave(T // 2)
            for j in range(KD):
                v.wait_ge(s_k1, j + 1)
                v.tensor_reduce(kneg1[:, j:j + 1], PS[:, 1536 * (j % 2):1536 * (j % 2) + N], AX.X, ALU.max,
                                negate=True).then_inc(s_k1m, 1)
            kT3 = kT1.rearrange("p (j n) -> p j n", j=KD)
            v.memset(kT3[:, :, N:NP], 0.0).then_inc(s_k1e, 1)
            with v.Fori(0, T // 2) as pair:
                link.enter(pair, 6)
                for k in range(2):
                    t = pair * 2 + k
                    v.wait_ge(s_q1e, t + 1)
                    qm = qm1[:, HEADS * k:HEADS * k + HEADS]
                    qr = QR[:, ds(t * D, D)].rearrange("p (h c) -> p h c", h=HEADS)
                    link(v.tensor_reduce(qm, qr, AX.X, ALU.add))
                    link(v.reciprocal(qm, qm))
                    link(v.tensor_scalar(qm, qm, 64 ** -0.5, None, ALU.mult))
                    v.tensor_tensor(qr, qr, qm.unsqueeze(2).to_broadcast([P, HEADS, 64]), ALU.mult).then_inc(s_q1n, 1)
            link.leave(T // 2)
            v.wait_ge(s_k1e, KD + 1)
            link(v.reciprocal(ksum1, ksum1))
            v.wait_ge(s_po2, 4)
            v.wait_ge(s_cx, 1)
            v.tensor_tensor(ctxT.rearrange("p (j c) -> p j c", j=KD), bank(2).rearrange("p (j c) -> p j c", j=KD),
                            bmask.unsqueeze(1).to_broadcast([P, KD, P]), ALU.mult).then_inc(s_cxc, 1)
            for j in range(KD):
                v.wait_ge(s_m1, j + 1)
                v.tensor_scalar(M1[:, D * j:D * j + D], bank(3 + j % 2), ksum1[:, j:j + 1], None, ALU.mult).then_inc(s_m1c, 1)
            with v.Fori(0, T) as t:
                v.wait_ge(s_moc, t + 1)
                link.enter(t, 1)
                link(v.bn_stats(stat[:, ds(t * 6, 6)], MO[:, ds(t * D, D)]))
            link.leave(T)
            for t in range(T):
                last = v.bn_aggr(mv[:, 2 * t:2 * t + 2], stat[:, 6 * t:6 * t + 6])
            last.then_inc(s_var1, 1)
            v.wait_ge(s_sd1, 1)
            link(v.reciprocal(rstd, rstd2))
            with v.Fori(0, T) as t:
                mo = MO[:, ds(t * D, D)]
                link.enter(t, 1)
                link(v.scalar_tensor_tensor(mo, mo, mv[:, ds(t * 2, 1)], gam, ALU.subtract, ALU.mult))
                v.scalar_tensor_tensor(X[:, ds(t * D, D)], mo, rstd[:, ds(t, 1)], X[:, ds(t * D, D)], ALU.mult, ALU.add)
            link.leave(T)
            stage_barrier(v, 3)
            if last_stage == 3:
                return
            statistics(X, 3)
            normalise(3)
            v.wait_ge(s_xn[3], T)

            def head_keys(t, h):
                v.wait_ge(s_sc4, t * PH + (h + 1))
                v.sem_inc(s_passed[1], 1)
                half = [bank(2 + 2 * (h % 2) + c, NK) for c in range(2)]
                cols = [slice(16 * h + 8 * c, 16 * h + 8 * c + 8) for c in range(2)]
                v.max(s8[:, cols[0]], half[0])
                link(v.max(s8[:, cols[1]], half[1]))
                v.sem_inc(s_passed[1], 1)
                v.max_index(i8[:, cols[0]], s8[:, cols[0]], half[0])
                v.max_index(i8[:, cols[1]], s8[:, cols[1]], half[1]).then_inc(s_scf, 1)

            def pair_scores(t):
                v.wait_ge(s_scf, t * PH + (PH + 2))
                s4 = s8.rearrange("p (h c k) -> p h c k", h=PH, c=2)
                c4 = comb.rearrange("p (h a b) -> p h a b", h=PH, a=TK)
                link(v.tensor_tensor(c4, s4[:, :, 0, :].unsqueeze(3).to_broadcast([P, PH, TK, TK]),
                                     s4[:, :, 1, :].unsqueeze(2).to_broadcast([P, PH, TK, TK]), ALU.add))
                v.sem_inc(s_passed[1], 1)
                for h in range(PH):
                    last = v.max(v8[:, 8 * h:8 * h + 8], comb[:, 64 * h:64 * h + 64])
                link(last)
                v.sem_inc(s_passed[1], 1)
                for h in range(PH):
                    last = v.max_index(pos[:, 8 * h:8 * h + 8], v8[:, 8 * h:8 * h + 8], comb[:, 64 * h:64 * h + 64])
                link(last)

            def row_numbers(t, k):
                link(v.tensor_copy(i8f, i8))
                link(v.tensor_scalar(posa, pos, 3, None, ALU.logical_shift_right))
                link(v.tensor_scalar(posb, pos, 7, None, ALU.bitwise_and))
                link(v.tensor_copy(posf[:, 0:64], posa))
                link(v.tensor_copy(posf[:, 64:128], posb))
                i4 = i8f.rearrange("p (h c k) -> p h c k", h=PH, c=2)
                e3 = eqk.rearrange("p (g j) -> p g j", j=TK)
                e4 = eqk.rearrange("p (h k j) -> p h k j", h=PH, k=TK)
                for c in range(2):
                    link(v.tensor_tensor(e3, posf[:, 64 * c:64 * c + 64].unsqueeze(2).to_broadcast([P, 64, TK]),
                                         iota8.unsqueeze(1).to_broadcast([P, 64, TK]), ALU.is_equal))
                    link(v.tensor_tensor(e4, e4, i4[:, :, c, :].unsqueeze(2).to_broadcast([P, PH, TK, TK]), ALU.mult))
                    link(v.tensor_reduce(isel[:, 64 * c:64 * c + 64], e3, AX.X, ALU.add))
                v.scalar_tensor_tensor(rowid[k], isel[:, 0:64], float(NK), isel[:, 64:128],
                                       ALU.mult, ALU.add).then_inc(s_rows, 1)
                sv = soft[k].rearrange("p (h k) -> p h k", h=PH)
                vv = v8.rearrange("p (h k) -> p h k", h=PH)
                v.tensor_tensor(sv, vv, vv[:, :, 0:1].to_broadcast([P, PH, TK]), ALU.subtract).then_inc(s_sub4, 1)

            def score_weights(t, k):
                v.wait_ge(s_exp4, t + 1)
                sv = soft[k].rearrange("p (h k) -> p h k", h=PH)
                link(v.tensor_reduce(smax, sv, AX.X, ALU.add))
                link(v.reciprocal(smax, smax))
                link(v.tensor_tensor(sv, sv, smax.unsqueeze(2).to_broadcast([P, PH, TK]), ALU.mult))
                link(v.tensor_copy(xcur[k], XN[:, ds(t * D, D)]))

            def down_products(t, k, more, first):
                for h in range(PH):
                    for g in range(TK * h, TK * h + TK):
                        v.wait_ge(s_gat[g % SLOTS], t * (16 * GPT // SLOTS) + 16 * (g // SLOTS + 1))
                        down = slot[g % SLOTS][:, 0:D]
                        last = v.tensor_tensor_reduce(out=down, in0=xcur[k], in1=down, scale=1.0,
                                                      scalar=0.0, op0=ALU.mult, op1=ALU.add,
                                                      accum_out=inner[:, g:g + 1])
                    link(last)
                    v.scalar_tensor_tensor(vals[:, TK * h:TK * h + TK], inner[:, TK * h:TK * h + TK], 0.0,
                                           soft[k][:, TK * h:TK * h + TK], ALU.max, ALU.mult).then_inc(s_vals, 1)
                    if more and h < 4:
                        head_keys(t + 1, 2 * h)
                        head_keys(t + 1, 2 * h + 1)
                    if more and h == 4:
                        pair_scores(t + 1)
                    if more and h == 5:
                        row_numbers(t + 1, 1 - k)
                    if more and h == 7:
                        score_weights(t + 1, 1 - k)

            def add_output(t, k):
                v.wait_ge(s_slot, t * GPT + (GPT + SLOTS))
                v.tensor_tensor(X[:, ds(t * D, D)], bank(6 + k), X[:, ds(t * D, D)], ALU.add).then_inc(s_xo, 1)

            for h in range(PH):
                head_keys(0, h)
            pair_scores(0)
            row_numbers(0, 0)
            score_weights(0, 0)
            LINKS = 2 * (PH + PH + 3 + 11 + 4)
            with v.Fori(0, T // 2 - 1) as pair:
                link.enter(pair, LINKS)
                for k in range(2):
                    down_products(pair * 2 + k, k, True, k == 0)
                    add_output(pair * 2 + k, k)
            link.leave(T // 2 - 1)
            down_products(T - 2, 0, True, False)
            add_output(T - 2, 0)
            down_products(T - 1, 1, False, False)
            add_output(T - 1, 1)

        @block.tensor
        def _(pe):
            mm = pe.matmul

            def transposes(l):
                for t in range(T):
                    pe.wait_ge(s_xn[l], t + 1)
                    if t >= 2:
                        pe.wait_ge(s_xt[l], t - 1)
                    for i in range(KD):
                        last = pe.transpose(bank(t % 2, P, start=P * i), XN[:, t * D + P * i:t * D + P * i + P], ident[:, :])
                    last.then_inc(s_xtp[l], 1)

            pe.wait_ge(s_const, CONSTANTS)
            pe.wait_ge(s_mm, 1)
            for c in range(3):
                last = pe.transpose(bank(0, P, start=P * c), dstf[:, P * c:P * c + P], ident[:, :])
            last.then_inc(s_pe1, 1)
            pe.wait_ge(s_mm, 2)
            mm(bank(1, NBP, NW), ones[:, 0:NW], dmin, start=True, stop=True)
            mm(bank(2, NBP, NW), ones[:, 0:NW], dmax, start=True, stop=True).then_inc(s_pe1, 1)
            pe.wait_ge(s_mm, 3)
            mm(bank(3, 1, NW), tri, wcnt, start=True, stop=True).then_inc(s_pe1, 1)
            pe.wait_ge(s_mm, 4)
            mm(bank(4, 3 * NW, 1), ones[0:NW, 0:1], flat3, start=True, stop=True).then_inc(s_pe1, 1)
            transposes(0)
            pe.wait_ge(s_w0, 16 * 13)
            wf = bank(5, 256).rearrange("p (i q j c) -> p i q j c", i=KD, q=2, j=KD)
            qk = bank(6, 64, 1).rearrange("p (q j c) -> p q j c", q=2, j=KD)
            bq = bdqk.rearrange("p (q c) -> p q c", q=2)
            for j in range(KD):
                for i in range(KD):
                    mm(wf[:, i, :, j, :], WinT[:, 512 * j + P * i:512 * j + P * i + P], bq, start=True, stop=True)
                last = mm(qk[:, :, j, :], binc[:, j:j + 1], bq, start=True, stop=True)
            last.then_inc(s_pe1, 1)
            pe.wait_ge(s_xt[0], T)
            pe.wait_ge(s_bound, 1)
            for j in range(KD):
                mm(bank(j), bdv, Wout[:, 512 * j:512 * j + 512], start=True, stop=True).then_inc(s_pe1, 1)
            pe.wait_ge(s_mm, 4 + 2 + 4)
            for t in range(T):
                if t >= 2:
                    pe.wait_ge(s_zc, t - 1)
                for i in range(KD):
                    last = mm(bank(t % 2), XNT3[:, i, P * t:P * t + P], W0[:, 512 * i:512 * i + 512],
                              start=i == 0, stop=i == KD - 1)
                last.then_inc(s_z, 1)
            for t in range(T):
                for i in range(KD):
                    mm(bank(6, HR, start=HR * t), XNT3[:, i, P * t:P * t + P], WF[:, 64 * i:64 * i + HR],
                       start=i == 0, stop=False)
                last = mm(bank(6, HR, start=HR * t), ones[0:1, 0:P], qkb[:, 0:HR], start=False, stop=True)
            last.then_inc(s_pe1, 1)
            for c, (c0, cn) in enumerate(CHUNKS):
                for i in range(KD):
                    mm(bank(2 + c, cn, HR), WF[:, 64 * i + HR:64 * i + 64], XNT3[:, i, c0:c0 + cn],
                       start=i == 0, stop=False)
                for a in range(0, cn, P):
                    last = mm(bank(2 + c, P, HR, start=a), qkb[:, HR:64], ones[0:1, 0:P], start=False, stop=a == cn - P)
            last.then_inc(s_pe1, 1)
            pe.wait_ge(s_mm, 12)
            pe.wait_ge(s_kexp, 1)
            for t in range(T):
                last = pe.transpose(PS[0:HR, 1024 + P * t:1024 + P * t + P], qrow[:, HR * t:HR * t + HR], ident[:, :])
            last.then_inc(s_pe1, 1)
            for t in range(T):
                last = pe.transpose(bank(6, HR, start=HR * t), kTe[:, P * t:P * t + P], ident[0:HR, 0:HR])
            last.then_inc(s_pe1, 1)
            pe.wait_ge(s_mm, 14)
            for i in range(KD):
                for t in range(T):
                    last = mm(bank(7, HR, start=HR * i), XN[:, t * D + P * i:t * D + P * i + P],
                              krow[:, HR * t:HR * t + HR], start=t == 0, stop=t == T - 1)
            last.then_inc(s_pe1, 1)
            pe.wait_ge(s_mm, 15)
            for i in range(KD):
                last = mm(bank(5, 512, HR), kxT[:, HR * i:HR * i + HR], Win[:, 512 * i:512 * i + 512],
                          start=i == 0, stop=i == KD - 1)
            last.then_inc(s_pe1, 1)
            mm(bank(4, 512, HR), ones[0:1, 0:HR], binr, start=True, stop=True).then_inc(s_pe1, 1)
            pe.wait_ge(s_mm, 16)
            for j in range(KD):
                last = pe.transpose(bank(7, HR, start=HR * j), kxm[:, P * j:P * j + P], ident[0:HR, 0:HR])
            last.then_inc(s_pe1, 1)
            pe.wait_ge(s_mm, 17)
            for j in range(KD):
                last = mm(bank(5, 512, HR), kxmT[:, HR * j:HR * j + HR], VO[:, 512 * j:512 * j + 512],
                          start=j == 0, stop=j == KD - 1)
            last.then_inc(s_pe1, 1)
            pe.wait_ge(s_mm, 18)
            pe.wait_ge(s_zc, T)
            for t in range(T):
                if t >= 2:
                    pe.wait_ge(s_mixa, t - 1)
                mm(bank(t % 2), qTs[:, P * t:P * t + P], Mx, start=True, stop=False)
                mm(bank(t % 2), ones[0:1, 0:P], boutr, start=False, stop=True).then_inc(s_mix, 1)
            stage_barrier(pe, 0)
            pe.sem_inc(s_ohf, OHB)
            pe.sem_inc(s_stf, 2)
            pe.sem_inc(s_wevac, 2)
            pe.wait_ge(s_ohr, 1)
            with pe.Fori(0, NW // 2) as pair:
                for k in range(2):
                    w = pair * 2 + k
                    begin, end, lower = window_bounds(pe, w)
                    pe.wait_ge(s_wevac, w + 1)
                    for b3 in range(3):
                        mm(bank(3 * k + b3, P), zero_b, zero_b, start=True, stop=False, skip_group_check=True)
                    with pe.Fori(begin, end, OHB) as place:
                        for o in range(OHB):
                            pe.wait_ge(s_ohr, place + (o + 2))
                            pe.wait_ge(s_odr, place + (o + 1))
                            for s in range(T):
                                last = mm(PS[:, 1536 * k + P * s:1536 * k + P * s + P], ohs[o][:, P * s:P * s + P],
                                          ohd[o], start=False, stop=False, skip_group_check=True)
                            last.then_inc(s_ohf, 1)
                    for b3 in range(3):
                        last = mm(bank(3 * k + b3, P), zero_b, zero_b, start=False, stop=True, skip_group_check=True)
                    last.then_inc(s_win, 1)
            pe.wait_ge(s_stf, NW + 2)
            for t in range(T):
                if t >= 2:
                    pe.wait_ge(s_agga, t - 1)
                for s in range(T):
                    last = mm(bank(6 + t % 2), A0[:, NP * s + P * t:NP * s + P * t + P], ZF[:, D * s:D * s + D],
                              start=s == 0, stop=s == T - 1)
                last.then_inc(s_agg, 1)
            stage_barrier(pe, 1)
            if last_stage == 1:
                return
            transposes(1)
            pe.wait_ge(s_xt[1], T)
            pe.wait_ge(s_moew, 32)
            for c, (c0, cn) in enumerate(CHUNKS):
                for i in range(KD):
                    last = mm(bank(2 + c, cn, NE), wr[:, NE * i:NE * i + NE], XNT3[:, i, c0:c0 + cn],
                              start=i == 0, stop=i == KD - 1)
            last.then_inc(s_lg, 1)
            pe.wait_ge(s_ro, 1)
            pe.wait_ge(s_jc, 3)
            for c, (c0, cn) in enumerate(CHUNKS):
                last = mm(bank(2 + c, cn), erep, prob[:, c0:c0 + cn], start=True, stop=True)
            last.then_inc(s_lg, 1)
            mm(bank(6, P), erep, erep, start=True, stop=True).then_inc(s_es, 1)
            pe.wait_ge(s_esc, 1)
            with pe.Fori(0, ROUNDS) as r:
                pe.wait_ge(s_ok, r + 1)
                mm(bank(5, 1), esame, okc, start=True, stop=True).then_inc(s_oks, 1)
            pe.wait_ge(s_ro, 2)
            for t in range(T):
                last = pe.transpose(bank(2, NE, start=NE * t), prob[:, P * t:P * t + P], ident[0:NE, 0:NE])
            last.then_inc(s_lg, 1)
            pe.wait_ge(s_ro, 3)
            pe.sem_inc(s_oa, 5)
            pe.sem_inc(s_gelu, 3)
            pe.sem_inc(s_oy, 1)
            for t in range(T):
                pe.wait_ge(s_oa, t + 1)
                mm(bank(3 + t % 5), prob[:, P * t:P * t + P], b2, start=True, stop=True).then_inc(s_oy, 1)

            def hidden(e, k, turn):
                pe.wait_ge(s_ew[k], turn * 48 + 48)
                for u, (f, (c0, cn)) in enumerate([(f, c) for f in range(FB) for c in CHUNKS]):
                    pe.wait_ge(s_gelu, e * 6 + (u + 1))
                    for i in range(KD):
                        last = mm(bank(u % 3, cn), EW[k][:, FF * i + P * f:FF * i + P * f + P],
                                  XNT3[:, i, c0:c0 + cn], start=i == 0, stop=i == KD - 1)
                    last.then_inc(s_h, 1)

            def expert_output(e, k):
                pe.wait_ge(s_gelu, e * 6 + 9)
                for t in range(T):
                    pe.wait_ge(s_oa, e * T + (T + t + 1))
                    for f in range(FB):
                        last = mm(bank(3 + t % 5), hT[k][:, NP * f + P * t:NP * f + P * t + P],
                                  EW[k][:, 1024 + D * f:1024 + D * f + D], start=f == 0, stop=f == FB - 1)
                    last.then_inc(s_oy, 1)

            hidden(0, 0, 0)
            with pe.Fori(0, NE // 2 - 1) as pair:
                hidden(pair * 2 + 1, 1, pair)
                expert_output(pair * 2, 0)
                hidden(pair * 2 + 2, 0, pair + 1)
                expert_output(pair * 2 + 1, 1)
            hidden(NE - 1, 1, NE // 2 - 1)
            expert_output(NE - 2, 0)
            expert_output(NE - 1, 1)
            stage_barrier(pe, 2)
            if last_stage == 2:
                return
            pe.wait_ge(s_w1, 16 * 6)
            mm(bank(7), ones[0:1, 0:P], gamr, start=True, stop=True)
            mm(bank(6), ones[0:1, 0:P], br1, start=True, stop=True)
            mm(bank(5, 1), ones[0:1, 0:P], alr, start=True, stop=True).then_inc(s_bc, 1)
            transposes(2)
            pe.wait_ge(s_xt[2], T)
            for t in range(T):
                if t >= 2:
                    pe.wait_ge(s_yc, t - 1)
                for i in range(KD):
                    last = mm(bank(t % 2), XNT3[:, i, P * t:P * t + P], Wg1[:, D * i:D * i + D],
                              start=i == 0, stop=i == KD - 1)
                last.then_inc(s_y, 1)
            pe.wait_ge(s_dsum, 1)
            for t in range(T):
                last = mm(bank(4, 1, start=t), a1sum[:, P * t:P * t + P], ones[:, 0:1], start=True, stop=True)
            last.then_inc(s_deg, 1)
            pe.wait_ge(s_yc, T)
            for t in range(T):
                if t >= 2:
                    pe.wait_ge(s_agga1, t - 1)
                for s in range(T):
                    last = mm(bank(2 + t % 2), A0[:, NP * s + P * t:NP * s + P * t + P], ZF[:, D * s:D * s + D],
                              start=s == 0, stop=s == T - 1)
                last.then_inc(s_agg1, 1)
            pe.wait_ge(s_bcc, 1)
            Wq3 = Wqkv.rearrange("p (i n) -> p i n", i=KD)
            for t in range(T):
                if t >= 2:
                    pe.wait_ge(s_q1s, t - 1)
                for i in range(KD):
                    last = mm(bank(6 + t % 2), XNT3[:, i, P * t:P * t + P], Wq3[:, i, 0:D],
                              start=i == 0, stop=i == KD - 1)
                last.then_inc(s_q1, 1)
            pe.wait_ge(s_agga1, T)
            for j in range(KD):
                if j >= 2:
                    pe.wait_ge(s_k1e, j)
                for c, (c0, cn) in enumerate(CHUNKS):
                    for i in range(KD):
                        last = mm(bank(3 * (j % 2) + c, cn), Wq3[:, i, D + P * j:D + P * j + P],
                                  XNT3[:, i, c0:c0 + cn], start=i == 0, stop=i == KD - 1)
                last.then_inc(s_k1, 1)
            pe.wait_ge(s_q1s, T)
            for t in range(T):
                if t >= 2:
                    pe.wait_ge(s_v1c, t - 1)
                for i in range(KD):
                    last = mm(bank(6 + t % 2), XNT3[:, i, P * t:P * t + P], Wq3[:, i, 2 * D:3 * D],
                              start=i == 0, stop=i == KD - 1)
                last.then_inc(s_v1, 1)
            pe.wait_ge(s_k1e, KD + 1)
            for t in range(T):
                if t >= 2:
                    pe.wait_ge(s_krc, t - 1)
                for j in range(KD):
                    last = pe.transpose(bank(t % 2, P, start=P * j), kT1[:, NP * j + P * t:NP * j + P * t + P], ident[:, :])
                last.then_inc(s_kr, 1)
            pe.wait_ge(s_krc, T)
            pe.wait_ge(s_v1c, T)
            for j in range(KD):
                for t in range(T):
                    last = mm(bank(2, P, start=P * j), V1[:, D * t + P * j:D * t + P * j + P],
                              kR1[:, D * t + P * j:D * t + P * j + P], start=t == 0, stop=t == T - 1)
            last.then_inc(s_cx, 1)
            pe.wait_ge(s_cxc, 1)
            for j in range(KD):
                if j >= 2:
                    pe.wait_ge(s_m1c, j - 1)
                mm(bank(3 + j % 2), ctxT[:, P * j:P * j + P], Wo1[:, D * j:D * j + D],
                   start=True, stop=True).then_inc(s_m1, 1)
            pe.wait_ge(s_q1n, T)
            for t in range(T):
                if t >= 2:
                    pe.wait_ge(s_qtc, t - 1)
                for j in range(KD):
                    last = pe.transpose(bank(t % 2, P, start=P * j), QR[:, D * t + P * j:D * t + P * j + P], ident[:, :])
                last.then_inc(s_qt, 1)
            pe.wait_ge(s_qtc, T)
            pe.wait_ge(s_m1c, KD)
            for t in range(T):
                if t >= 2:
                    pe.wait_ge(s_moc, t - 1)
                for j in range(KD):
                    last = mm(bank(6 + t % 2), qT1[:, NP * j + P * t:NP * j + P * t + P], M1[:, D * j:D * j + D],
                              start=j == 0, stop=j == KD - 1)
                last.then_inc(s_mo, 1)
            stage_barrier(pe, 3)
            if last_stage == 3:
                return
            transposes(3)
            pe.wait_ge(s_xt[3], T)
            pe.wait_ge(s_w4, 48)
            pe.sem_inc(s_scf, 2)
            pe.sem_inc(s_slot, SLOTS)

            def queries(t):
                for h in range(PH):
                    for i in range(KD):
                        last = mm(bank(h // 4, P, start=P * (h % 4)), Wq4[:, 1024 * i + P * h:1024 * i + P * h + P],
                                  XNT3[:, i, ds(t * P, P)], start=i == 0, stop=i == KD - 1)
                    if h % 4 == 3:
                        last.then_inc(s_q4, 1)

            def scores(t, h):
                pe.wait_ge(s_q4c, t * PH + (h + 1))
                pe.wait_ge(s_scf, t * PH + (h + 1))
                for c in range(2):
                    rows = slice(64 * c, 64 * c + 64)
                    last = mm(bank(2 + 2 * (h % 2) + c, NK), qT4[rows, P * h:P * h + P],
                              keysT[rows, NK * h:NK * h + NK], start=True, stop=True)
                last.then_inc(s_sc4, 1)

            def up_products(t, k, more):
                if more:
                    pe.wait_ge(s_q4c, (t + 1) * PH)
                    queries(t + 1)
                for h in range(PH):
                    if more and h < 4:
                        scores(t + 1, 2 * h)
                        scores(t + 1, 2 * h + 1)
                    for g in range(TK * h, TK * h + TK):
                        pe.wait_ge(s_dg, t * GPT + (g + 1))
                        last = mm(bank(6 + k), diag[g % 4], slot[g % SLOTS][:, D:2 * D],
                                  start=g == 0, stop=g == GPT - 1)
                        last.then_inc(s_slot, 1)

            queries(0)
            for h in range(PH):
                scores(0, h)
            with pe.Fori(0, T // 2 - 1) as pair:
                for k in range(2):
                    up_products(pair * 2 + k, k, True)
            up_products(T - 2, 0, True)
            up_products(T - 1, 1, False)


_OUT = (N, D)


def _layout(inputs):
    import numpy as np
    a = {k: np.asarray(v) for k, v in inputs.items()}
    pad = NBP * P - EDGES

    def edges(e, fill):
        e = np.concatenate([e, np.full(pad, fill, e.dtype)])
        return np.ascontiguousarray(e.reshape(NBP, P).T)

    x = np.concatenate([a["x"], np.zeros((NP - N, D), a["x"].dtype)])
    got = {
        "x": x,
        "src": edges(a["src"], NP - 1), "dst": edges(a["dst"], NP - 1),
        "edge_weight": edges(a["edge_weight"], 0),
        "L0_gnn_W": a["L0_gnn_W"], "L0_mix_W_in": a["L0_mix_W_in"], "L0_mix_W_in_T": a["L0_mix_W_in"].T,
        "L0_mix_W_q": a["L0_mix_W_q"], "L0_mix_W_k": a["L0_mix_W_k"], "L0_mix_W_v_T": a["L0_mix_W_v"].T,
        "L0_mix_W_out": a["L0_mix_W_out"], "L0_mix_b_in": a["L0_mix_b_in"],
        "L0_ffn_Wr": a["L0_ffn_Wr"].reshape(KD, P, NE).transpose(1, 0, 2).reshape(P, KD * NE),
        "L0_ffn_b1_col": a["L0_ffn_b1"].reshape(NE * FB, P).T, "L0_ffn_b2": a["L0_ffn_b2"],
        "L0_ffn_W1": a["L0_ffn_W1"], "L0_ffn_W2": a["L0_ffn_W2"],
        "L1_gnn_W_T": a["L1_gnn_W"].T, "L1_gnn_b": a["L1_gnn_b"], "L1_gnn_alpha": a["L1_gnn_alpha"].reshape(1),
        "L1_mix_w_qkv_T": a["L1_mix_w_qkv"].T, "L1_mix_w_out_T": a["L1_mix_w_out"].T, "L1_mix_gamma": a["L1_mix_gamma"],
        "L1_ffn_Wq": a["L1_ffn_Wq"], "L1_ffn_bq_col": a["L1_ffn_bq"].reshape(PH, P).T,
        "L1_ffn_keys_T": a["L1_ffn_keys"].transpose(0, 1, 3, 2).reshape(PH, P, NK),
        "L1_ffn_w": np.concatenate([a["L1_ffn_w_down"], a["L1_ffn_w_up"]], axis=1),
        "L0_mix_b_in_col": a["L0_mix_b_in"].reshape(KD, P).T, "L0_mix_b_out": a["L0_mix_b_out"],
    }
    return {k: np.ascontiguousarray(v) for k, v in got.items()}


def kernel(**inputs):
    import concourse.bacc as _bacc
    from concourse.bass_utils import run_bass_kernel_spmd as _run

    nc = _bacc.Bacc("TRN2", target_bir_lowering=False, num_devices=1)
    arrays, aps = {}, {}
    for name, a in _layout(inputs).items():
        arrays[f"in_{name}_dram"] = a
        aps[name] = nc.dram_tensor(f"in_{name}_dram", a.shape, mybir.dt.from_np(a.dtype), kind="ExternalInput").ap()
    out = nc.dram_tensor("out_0_dram", _OUT, F32, kind="ExternalOutput").ap()
    gps_two_layers(nc, aps, out, LAST_STAGE)
    r = _run(nc, [arrays], core_ids=[0])
    return r.results[0]["out_0_dram"]


LAST_STAGE = 4
```

```python
import concourse.bass as bass
from concourse import mybir
from contextlib import ExitStack

F32 = mybir.dt.float32
BF16 = mybir.dt.bfloat16
I32 = mybir.dt.int32
U32 = mybir.dt.uint32
I16 = mybir.dt.int16
U16 = mybir.dt.uint16
ALU = mybir.AluOpType
ACT = mybir.ActivationFunctionType
AX = mybir.AxisListType
ds = bass.ds

N = 1250
D = 512
P = 128
T = (N + P - 1) // P
NP = T * P
TAIL = N - (T - 1) * P
KD = D // P
CHUNKS = [(0, 512), (512, 512), (1024, 256)]
EDGES = 41250
NB = (EDGES + P - 1) // P
NBP = 3 * P
WIN = 32
NW = NP // WIN
EQ0 = 2944
WSTEP = 2048
assert NP <= WSTEP and WSTEP * NW < 1 << 24
OHB = 3
NBE = NB + OHB - 1
NBV = NBE + OHB - 1
TURNS = (NB + OHB - 1) // OHB
FIRST_BITS, TURN_BITS = 9, 7
assert NB <= 1 << FIRST_BITS and TURNS < 1 << TURN_BITS and TURNS * NW < 1 << 30 - FIRST_BITS - TURN_BITS
HEADS = 8
KR = 4
HR = HEADS * KR
NE = 8
FF = 256
FB = FF // P
CAP = 512
ROUNDS = 8
PH = 8
NK = 256
TK = 8
GPT = PH * TK
SLOTS = 16
EPS = 1e-5
CONSTANTS = 18


class Chain:

    def __init__(self, engine, sem):
        self.engine, self.sem, self.n, self.base = engine, sem, 0, 0

    def __call__(self, instruction):
        instruction.then_inc(self.sem, 1)
        self.n += 1
        self.engine.wait_ge(self.sem, self.base + self.n)

    def enter(self, turn, links):
        self.outer = self.base + self.n
        self.base, self.n = self.outer + turn * links, 0
        self.links = links

    def leave(self, turns):
        assert self.n == self.links
        self.base, self.n = self.outer + turns * self.links, 0


def gps_two_layers(nc, d, out):
    ctx = ExitStack()
    with ctx:
        def sb(name, shape, dt=F32):
            return ctx.enter_context(nc.sbuf_tensor(name, shape, dt))

        def sem(name):
            return ctx.enter_context(nc.semaphore(name))

        X = sb("X", [P, T * D])
        XN = sb("XN", [P, T * D])
        XNT = sb("XNT", [P, KD * NP])
        XNT3 = XNT[:, :].rearrange("p (i n) -> p i n", i=KD)
        ARENA = sb("ARENA", [P, 5120 + 12800 + 6400])
        ZF = ARENA[:, 0:5120]
        A0 = ARENA[:, 5120:17920]
        A1C = ARENA[:, 17920:24320].bitcast(U16)
        WREG = sb("WREG", [P, 10240])
        edgef = sb("edgef", [P, 2 * NBP])
        dstf = edgef[:, 0:NBP]
        srcw = edgef[:, NBP:2 * NBP]
        iota32 = sb("iota32", [P, WIN])
        windows = sb("windows", [P, NW])
        wparts = sb("wparts", [P, NBP * 4], BF16)
        ident = sb("ident", [P, P])
        ones = sb("ones", [P, P])
        iota16 = sb("iota16", [P, NP], I16)
        small = sb("small", [P, 768])
        epsc = small[:, 0:1]
        stat = small[:, 8:68]
        mv = small[:, 68:88]
        rstd = small[:, 88:98]
        rstd2 = small[:, 98:108]
        degc = small[:, 108:118]
        adeg = small[:, 118:128]
        PS = ctx.enter_context(nc.psum_tensor("PS", [P, 4096], F32))

        def bank(b, n=512, p=P, start=0):
            return PS[0:p, 512 * b + start:512 * b + start + n]

        raw_dst = A0[:, 0:NBP].bitcast(I32)
        raw_src = A0[:, NBP:2 * NBP].bitcast(I32)
        raw_w = A0[:, 2 * NBP:3 * NBP]
        res1 = A0[:, 3 * NBP:4 * NBP]
        dmin = A0[:, 4 * NBP:5 * NBP]
        dmax = A0[:, 5 * NBP:6 * NBP]
        hit = A0[0:NW, 6 * NBP:7 * NBP]
        hitb = A0[0:NW, 7 * NBP:8 * NBP]
        bup = A0[0:NW, 8 * NBP:9 * NBP]
        bdown = A0[0:NW, 9 * NBP:10 * NBP]
        bthird = A0[0:NW, 10 * NBP:11 * NBP]
        flat3 = A0[0:NW, 11 * NBP:11 * NBP + 3 * NW]
        dlow = A0[:, 11 * NBP + 3 * NW:12 * NBP + 3 * NW]
        dtmp = A0[:, 12 * NBP + 3 * NW:13 * NBP + 3 * NW].bitcast(I32)
        blkmin = small[:, 128:131]
        blkmax = small[:, 131:134]
        winlo = small[0:NW, 134:135]
        winhi = small[0:NW, 135:136]
        wfirst = small[0:NW, 136:137]
        wend = small[0:NW, 137:138]
        woff = small[0:NW, 138:139]
        wcnt = small[0:NW, 139:140]
        tri = small[0:NW, 140:140 + NW]
        bounds3 = small[0:1, 180:180 + 3 * NW].bitcast(I32)
        bounds = small[0:1, 520:520 + NW].bitcast(I32)
        W0 = WREG[:, 0:2048]
        Win = WREG[:, 2048:4096]
        WinT = WREG[:, 4096:6144]
        Wout = WREG[:, 6144:8192]
        VO = WREG[:, 8192:10240]
        q0 = 5376
        WF = A0[:, q0:q0 + 256]
        bdqk = A0[:, q0 + 256:q0 + 272]
        bdv = A0[:, q0 + 272:q0 + 400]
        binc = A0[:, q0 + 400:q0 + 404]
        qkb = A0[0:1, q0 + 404:q0 + 468]
        headmask = A0[0:HR, q0 + 500:q0 + 1012]
        qrow = A0[:, q0 + 1012:q0 + 1332]
        krow = A0[:, q0 + 1332:q0 + 1652]
        qmax = A0[:, q0 + 1652:q0 + 1732]
        kxT = A0[:, q0 + 1732:q0 + 1860]
        kxm = A0[0:HR, q0 + 1860:q0 + 2372]
        kxr = kxm
        kxmT = A0[:, q0 + 2372:q0 + 2500]
        Mx = A0[0:HR, q0 + 2500:q0 + 3012]
        kTe = A0[0:HR, q0 + 3012:q0 + 3012 + NP]
        qTs = A0[0:HR, q0 + 4300:q0 + 4300 + NP]
        qlT = A0[HR:2 * HR, q0 + 4300:q0 + 4300 + NP]
        boutr = A0[0:1, q0 + 5600:q0 + 6112]
        binr = A0[0:1, q0 + 6112:q0 + 6624]
        ksum = small[0:HR, 320:321]
        kneg = small[0:HR, 321:322]
        ohs = [XNT[:, 640 * k:640 * k + 640].bitcast(BF16) for k in range(OHB)]
        ohd = [XNT[:, 1920 + 64 * k:1984 + 64 * k].bitcast(BF16) for k in range(OHB)]
        zero_b = XNT[:, 2112:2112 + 64].bitcast(BF16)
        staged = XNT[:, 2176:2176 + 2 * 960]
        summed = XNT[:, 4096:4096 + 2 * 320]
        eq32 = WREG[:, EQ0:EQ0 + NBV * WIN // 2].bitcast(BF16)
        EW = [WREG[:, 0:2048], WREG[:, 2048:4096]]
        hT = [ZF[:, 0:2560], ZF[:, 2560:5120]]
        prob = WREG[0:NE, 4096:5376]
        probR = WREG[:, 5376:6656]
        sel1 = WREG[:, 6656:7936]
        sel2 = WREG[:, 7936:9216]
        b2 = WREG[0:NE, 9312:9824]
        wr = WREG[:, 9824:9856]
        b1k = [WREG[:, 9856:9858], WREG[:, 9858:9860]]
        gate = WREG[:, 9860:9940]
        esame = WREG[:, 9940:10068]
        erep = WREG[0:NE, 10068:10196]
        jbits = small[:, 330:330 + ROUNDS].bitcast(I32)
        jcol = small[:, 340:341].bitcast(I32)
        jcl = small[:, 341:342].bitcast(I32)
        basei = small[:, 342:343].bitcast(I32)
        thri = small[:, 343:344].bitcast(I32)
        thrf = small[:, 343:344]
        cntc = small[:, 344:345]
        okc = small[:, 345:346]
        stepf = small[:, 346:347]
        stepi = small[:, 347:348].bitcast(I32)
        pneg = small[0:NE, 348:349]
        psumc = small[0:NE, 349:350]
        cgt = small[0:NE, 350:351]
        need = small[0:NE, 351:352]
        Wqkv = WREG[:, 4096:10240]
        Wg1 = WREG[:, 0:2048]
        Wo1 = WREG[:, 2048:4096]
        kT1 = A0[:, 0:5120]
        kR1 = A0[:, 5120:10240]
        ctxT = A0[:, 10240:10752]
        M1 = A0[:, 10752:12800]
        QR = ARENA[:, 17920:23040]
        bmask = ARENA[:, 23040:23168]
        qT1 = kT1
        MO = ARENA[:, 18432:23552]
        V1 = ZF
        gam = ARENA[:, 23552:24064]
        ab = QR[:, 4608:5120]
        kneg1 = small[:, 360:364]
        ksum1 = small[:, 364:368]
        alphac = small[:, 368:369]
        a1sum = QR[:, 0:NP]
        qm1 = small[:, 384:464]
        gamr = wparts[0:1, 0:1024].bitcast(F32)
        br1 = edgef[0:1, 0:D]
        alr = small[0:1, 369:370]
        Wq4 = WREG[:, 0:4096]
        keysT = WREG[:, 4096:6144]
        qT4 = WREG[:, 6144:7168]
        s8 = WREG[:, 7168:7296]
        i8 = WREG[:, 7296:7424].bitcast(U32)
        i8f = WREG[:, 7424:7552]
        comb = WREG[:, 7552:8064]
        v8 = WREG[:, 8064:8128]
        pos = WREG[:, 8128:8192].bitcast(U32)
        posa = WREG[:, 8192:8256].bitcast(U32)
        posb = WREG[:, 8256:8320].bitcast(U32)
        posf = WREG[:, 8320:8448]
        eqk = WREG[:, 8448:8960]
        isel = WREG[:, 8960:9088]
        rowid = [WREG[:, 9088 + 64 * k:9152 + 64 * k].bitcast(I32) for k in range(2)]
        soft = [WREG[:, 9216 + 64 * k:9280 + 64 * k] for k in range(2)]
        inner = WREG[:, 9344:9408]
        vals = WREG[:, 9408:9472]
        xcur = [ARENA[:, 16896 + 512 * k:17408 + 512 * k] for k in range(2)]
        xnext = [XN[:, 512 * k:512 * k + 512] for k in range(2)]
        diag = [ARENA[:, 17920 + 128 * k:18048 + 128 * k] for k in range(4)]
        slot = [ARENA[:, 1024 * k:1024 * k + 1024] for k in (0, 1, 2, 3, 4, 10, 11, 12, 13, 14, 5, 6, 7, 8, 9, 15)]
        iota8 = small[:, 470:478]
        bq4 = small[:, 480:488]
        smax = small[:, 488:496]
        scale2 = small[:, 500:500 + ROUNDS]
        stat1 = [small[:, 560 + 6 * k:566 + 6 * k] for k in range(2)]
        mv1 = [small[:, 572 + 2 * k:574 + 2 * k] for k in range(2)]
        dev1 = [small[:, 576 + k:577 + k] for k in range(2)]
        rstd1 = [small[:, 578 + k:579 + k] for k in range(2)]

        s_x = sem("x_loaded")
        s_edges = sem("edges_loaded")
        s_w0 = sem("layer0_weights_loaded")
        s_const = sem("constants_built")
        s_dv = sem("vector_chain")
        s_sc = sem("scalar_chain")
        s_po = sem("window_parts_added")
        s_masks = sem("masks_built")
        stage_end = [sem(f"stage_{k}_ended") for k in range(3)]
        s_var = [sem(f"variance_ready_{l}") for l in range(4)]
        s_sd = [sem(f"deviation_ready_{l}") for l in range(4)]
        s_xn = [sem(f"norm_ready_{l}") for l in range(4)]
        s_xtp = [sem(f"norm_transposed_{l}") for l in range(4)]
        s_xt = [sem(f"norm_transpose_copied_{l}") for l in range(4)]
        s_pe1 = sem("small_product_ready")
        s_bs = sem("bounds_operand_ready")
        s_bp = sem("bounds_product_ready")
        s_mm = sem("mixer_operand_ready")
        s_z = sem("z_tile_ready")
        s_zc = sem("z_tile_copied")
        s_qlc = sem("query_logits_copied")
        s_kx = sem("keys_times_norm_ready")
        s_kxc = sem("keys_times_norm_copied")
        s_kexp = sem("key_exponentials_ready")
        s_kneg = sem("key_maximum_ready")
        s_qsub = sem("query_shifted")
        s_qexp = sem("query_exponentials_ready")
        s_bo = sem("output_bias_broadcast")
        s_mix = sem("mix_tile_ready")
        s_mixa = sem("mix_tile_added")
        s_bound = sem("window_bounds_ready")
        s_ohr = sem("one_hot_sources_ready")
        s_odr = sem("weighted_destinations_ready")
        s_ohf = sem("one_hot_buffer_free")
        s_win = sem("window_summed")
        s_wevac = sem("window_banks_free")
        s_stg = sem("window_staged")
        s_stf = sem("window_stage_free")
        s_agg = sem("aggregate_ready")
        s_agga = sem("aggregate_added")
        s_moew = sem("expert_constants_loaded")
        s_ew1 = [sem(f"hidden_weights_loaded_{k}") for k in range(2)]
        s_ew2 = [sem(f"output_weights_loaded_{k}") for k in range(2)]
        s_lg = sem("router_product_ready")
        s_ro = sem("router_operand_ready")
        s_pm = sem("router_maximum_ready")
        s_pexp = sem("router_exponentials_ready")
        s_jc = sem("search_constants_built")
        s_es = sem("same_expert_mask_ready")
        s_esc = sem("same_expert_mask_copied")
        s_ok = sem("search_counts_ready")
        s_oks = sem("search_counts_summed")
        s_h = sem("hidden_product_ready")
        s_gelu = sem("hidden_ready")
        s_oy = sem("expert_product_ready")
        s_oa = sem("expert_product_added")
        s_w1 = sem("layer1_weights_loaded")
        s_w1m = sem("mixer_weights_loaded")
        s_bc = sem("rows_broadcast")
        s_bcc = sem("row_broadcasts_copied")
        s_y = sem("y_tile_ready")
        s_yc = sem("y_tile_copied")
        s_dsum = sem("degree_partial_ready")
        s_deg = sem("degree_ready")
        s_agg1 = sem("mean_aggregate_ready")
        s_agga1 = sem("mean_aggregate_added")
        s_q1 = sem("query_tile_ready")
        s_q1s = sem("query_tile_shifted")
        s_q1e = sem("query_tile_exponentials")
        s_q1n = sem("query_tile_normalised")
        s_k1 = sem("key_block_ready")
        s_k1m = sem("key_block_maximum")
        s_k1e = sem("key_block_exponentials")
        s_v1 = sem("value_tile_ready")
        s_v1c = sem("value_tile_copied")
        s_kr = sem("key_rows_ready")
        s_krc = sem("key_rows_copied")
        s_cx = sem("context_ready")
        s_cxc = sem("context_masked")
        s_m1 = sem("output_matrix_ready")
        s_m1c = sem("output_matrix_scaled")
        s_qt = sem("query_transposed")
        s_qtc = sem("query_transpose_copied")
        s_mo = sem("mixer_output_ready")
        s_moc = sem("mixer_output_copied")
        s_var1 = sem("mixer_variance_ready")
        s_sd1 = sem("mixer_deviation_ready")
        s_w4 = sem("product_key_weights_loaded")
        s_q4 = sem("head_query_ready")
        s_q4c = sem("head_query_copied")
        s_sc4 = sem("head_scores_ready")
        s_scf = sem("head_scores_free")
        s_rows = sem("row_numbers_ready")
        s_sub4 = sem("scores_shifted")
        s_exp4 = sem("score_exponentials_ready")
        s_gat = [sem(f"slot_{k}_gathered") for k in range(SLOTS)]
        s_slot = sem("slot_free")
        s_passed = [sem(f"waits_passed_{k}") for k in range(2)]
        s_vals = sem("head_values_ready")
        s_dg = sem("diagonal_ready")
        s_xo = sem("tile_output_added")
        s_st = sem("tile_stored")
        VALUES_AFTER = [range(0), range(0, 2), range(2, 4), range(4, T)]
        HIDDEN = [(f, c) for f in range(FB) for c in CHUNKS]
        block = ctx.enter_context(nc.Block())

        def stage_barrier(engine, k):
            engine.drain().then_inc(stage_end[k], 1)
            engine.wait_ge(stage_end[k], 5)

        def window_bounds(engine, w):
            word = engine.value_load(bounds[0:1, ds(w, 1)], min_val=0, max_val=(1 << 30) - 1)
            first = word & ((1 << FIRST_BITS) - 1)
            turns = (word // (1 << FIRST_BITS)) & ((1 << TURN_BITS) - 1)
            begin = held(engine, word // (1 << (FIRST_BITS + TURN_BITS)) * OHB, 0, NBE * NW - OHB)
            end = held(engine, begin + turns * OHB, 1, NBE * NW)
            lower = held(engine, begin - first, -NB, NBE * NW) if engine is not nc.tensor else None
            return begin, end, lower

        def held(engine, value, least, most):
            return engine.snap(engine.to_reg(value), min_val=least, max_val=most)

        def edge_block(place, lower):
            return (place - lower).with_bounds(min_val=0, max_val=NBE - 1)

        @block.sync
        def _(sp):
            xv = d["x"].rearrange("(t p) n -> p t n", p=P)
            sp.dma_start(X[:, :].rearrange("p (t n) -> p t n", t=T), xv).then_inc(s_x, 16)
            sp.dma_start(raw_dst, d["dst"]).then_inc(s_edges, 16)
            sp.dma_start(raw_src, d["src"]).then_inc(s_edges, 16)
            sp.dma_start(raw_w, d["edge_weight"]).then_inc(s_edges, 16)
            for dst, name in ((W0, "L0_gnn_W"), (Win, "L0_mix_W_in"), (WinT, "L0_mix_W_in_T"), (Wout, "L0_mix_W_out")):
                sp.dma_start(dst.rearrange("p (i n) -> p i n", i=KD),
                             d[name].rearrange("(i p) n -> p i n", p=P)).then_inc(s_w0, 16)
            sp.wait_ge(s_const, 1)
            for h2 in range(2):
                rows = slice(64 * h2, 64 * h2 + 64)
                sp.dma_start(bdqk[rows, 4 * h2:4 * h2 + 4], d["L0_mix_W_k"]).then_inc(s_w0, 16)
                sp.dma_start(bdqk[rows, 8 + 4 * h2:12 + 4 * h2], d["L0_mix_W_q"]).then_inc(s_w0, 16)
                sp.dma_start(bdv[rows, rows], d["L0_mix_W_v_T"]).then_inc(s_w0, 16)
            sp.dma_start(binc, d["L0_mix_b_in_col"]).then_inc(s_w0, 16)
            sp.dma_start(binr, d["L0_mix_b_in"].unsqueeze(0)).then_inc(s_w0, 16)
            sp.dma_start(boutr, d["L0_mix_b_out"].unsqueeze(0)).then_inc(s_w0, 16)
            stage_barrier(sp, 0)
            for dst, name in ((wr, "L0_ffn_Wr"), (b2, "L0_ffn_b2")):
                sp.dma_start(dst, d[name]).then_inc(s_moew, 16)
            w1v = d["L0_ffn_W1"].rearrange("e (i p) n -> p e i n", p=P)
            w2v = d["L0_ffn_W2"].rearrange("e (f p) n -> p e f n", p=P)

            b1v = d["L0_ffn_b1_col"].rearrange("p (e f) -> p e f", e=NE)

            def hidden_weights(e, k):
                sp.dma_start(EW[k][:, 0:1024].rearrange("p (e i n) -> p e i n", e=1, i=KD),
                             w1v[:, ds(e, 1)]).then_inc(s_ew1[k], 16)
                sp.dma_start(b1k[k].rearrange("p (e f) -> p e f", e=1), b1v[:, ds(e, 1)]).then_inc(s_ew1[k], 16)

            def output_weights(e, k):
                sp.dma_start(EW[k][:, 1024:2048].rearrange("p (e f n) -> p e f n", e=1, f=FB),
                             w2v[:, ds(e, 1)]).then_inc(s_ew2[k], 16)

            hidden_weights(0, 0)
            output_weights(0, 0)
            stage_barrier(sp, 1)
            hidden_weights(1, 1)
            output_weights(1, 1)

            def next_weights(e, k):
                sp.wait_ge(s_gelu, e * 6 + (3 - 6))
                hidden_weights(e, k)
                sp.wait_ge(s_oy, e * T + 1)
                output_weights(e, k)

            with sp.Fori(1, NE // 2) as pair:
                for k in range(2):
                    next_weights(pair * 2 + k, k)
            sp.wait_ge(s_oy, NE * T + 1)
            sp.dma_start(Wg1.rearrange("p (i n) -> p i n", i=KD),
                         d["L1_gnn_W_T"].rearrange("(i p) n -> p i n", p=P)).then_inc(s_w1, 16)
            for dst, name in ((gamr, "L1_mix_gamma"), (br1, "L1_gnn_b"), (alr, "L1_gnn_alpha")):
                sp.dma_start(dst, d[name].unsqueeze(0)).then_inc(s_w1, 16)
            stage_barrier(sp, 2)
            for dst, name in ((Wqkv, "L1_mix_w_qkv_T"), (Wo1, "L1_mix_w_out_T")):
                sp.dma_start(dst.rearrange("p (i n) -> p i n", i=KD),
                             d[name].rearrange("(i p) n -> p i n", p=P)).then_inc(s_w1m, 16)
            sp.wait_ge(s_m1, KD)
            sp.dma_start(Wq4.rearrange("p (i n) -> p i n", i=KD),
                         d["L1_ffn_Wq"].rearrange("(i p) n -> p i n", p=P)).then_inc(s_w4, 16)
            sp.dma_start(keysT.rearrange("p (h n) -> p h n", h=PH),
                         d["L1_ffn_keys_T"].rearrange("h p n -> p h n")).then_inc(s_w4, 16)
            sp.dma_start(bq4, d["L1_ffn_bq_col"]).then_inc(s_w4, 16)
            with sp.Fori(0, T - 1) as t:
                sp.wait_ge(s_xo, t + 1)
                sp.dma_start(out[ds(t * P, P), :], X[:, ds(t * D, D)]).then_inc(s_st, 16)
            sp.wait_ge(s_xo, T)
            sp.dma_start(out[(T - 1) * P:N, :], X[0:TAIL, (T - 1) * D:T * D]).then_inc(s_st, 16)
            sp.wait_ge(s_st, 16 * T)

        @block.gpsimd
        def _(pool):
            built = Chain(pool, s_const)
            built(pool.memset(A0[:, q0:q0 + 1012], 0.0))
            built(pool.memset(ident[:, :], 0.0))
            built(pool.memset(ones[:, :], 1.0))
            built(pool.memset(headmask, 1.0))
            built(pool.memset(epsc, EPS))
            built(pool.affine_select(out=ident[:, :], in_=ident[:, :], compare_op=ALU.not_equal, fill=1.0,
                                     base=0, pattern=[[-1, P]], channel_multiplier=1))
            built(pool.iota(iota16[:, :], [[1, NP]], base=0, channel_multiplier=0))
            built(pool.iota(winlo, [[0, 1]], base=0, channel_multiplier=WIN, allow_small_or_imprecise_dtypes=True))
            built(pool.iota(winhi, [[0, 1]], base=WIN - 1, channel_multiplier=WIN, allow_small_or_imprecise_dtypes=True))
            built(pool.iota(bup, [[1, NBP]], base=1, channel_multiplier=0, allow_small_or_imprecise_dtypes=True))
            built(pool.iota(bdown, [[-1, NBP]], base=NB, channel_multiplier=0, allow_small_or_imprecise_dtypes=True))
            built(pool.iota(bthird, [[OHB, NBP]], base=0, channel_multiplier=0, allow_small_or_imprecise_dtypes=True))
            built(pool.iota(windows[:, :], [[-WSTEP, NW]], base=0, channel_multiplier=0, allow_small_or_imprecise_dtypes=True))
            built(pool.iota(iota32[:, :], [[1, WIN]], base=0, channel_multiplier=0, allow_small_or_imprecise_dtypes=True))
            built(pool.memset(tri, 1.0))
            built(pool.affine_select(out=tri, in_=tri, compare_op=ALU.is_gt, fill=0.0,
                                     base=0, pattern=[[1, NW]], channel_multiplier=-1))
            hm = headmask.rearrange("p (h c) -> p h c", h=HEADS)
            built(pool.affine_select(out=hm, in_=hm, compare_op=ALU.is_ge, fill=0.0,
                                     base=0, pattern=[[-KR, HEADS], [0, 64]], channel_multiplier=1))
            built(pool.affine_select(out=hm, in_=hm, compare_op=ALU.is_ge, fill=0.0,
                                     base=KR - 1, pattern=[[KR, HEADS], [0, 64]], channel_multiplier=-1))
            assert built.n == CONSTANTS
            stage_barrier(pool, 0)
            A0v = A0.rearrange("p (s n) -> p s n", s=T)

            def destinations(w):
                begin, end, lower = window_bounds(pool, w)
                with pool.Fori(begin, end, OHB) as place:
                    for k in range(OHB):
                        b = edge_block(place + k, lower)
                        pool.wait_ge(s_ohf, place + (k + 1))
                        pool.tensor_tensor(ohd[k].rearrange("p (q c) -> p q c", q=4),
                                           eq32[:, ds(b * WIN, WIN)].unsqueeze(1).to_broadcast([P, 4, WIN]),
                                           wparts[:, ds(b * 4, 4)].unsqueeze(2).to_broadcast([P, 4, WIN]),
                                           ALU.mult).then_inc(s_odr, 1)

            def add_parts(w, k):
                st = staged[:, 960 * k:960 * k + 960].rearrange("p (s q c) -> p s q c", s=T, q=3)
                tmp = summed[:, 320 * k:320 * k + 320].rearrange("p (s c) -> p s c", s=T)
                pool.wait_ge(s_stg, w + 1)
                pool.tensor_tensor(tmp, st[:, :, 0, :], st[:, :, 1, :], ALU.add).then_inc(s_po, 1)
                pool.wait_ge(s_po, w + 1)
                pool.tensor_tensor(A0v[:, :, ds(w * WIN, WIN)], tmp, st[:, :, 2, :], ALU.add).then_inc(s_stf, 1)

            destinations(0)
            with pool.Fori(0, NW // 2 - 1) as pair:
                for k in range(2):
                    destinations(pair * 2 + (k + 1))
                    add_parts(pair * 2 + k, k)
            destinations(NW - 1)
            add_parts(NW - 2, 0)
            add_parts(NW - 1, 1)
            stage_barrier(pool, 1)
            jb = Chain(pool, s_jc)
            jb(pool.iota(jcol, [[0, 1]], base=0, channel_multiplier=1))
            jb(pool.memset(erep, 1.0))
            er = erep.rearrange("p (j e) -> p j e", e=NE)
            jb(pool.affine_select(out=er, in_=er, compare_op=ALU.is_equal, fill=0.0,
                                  base=0, pattern=[[0, P // NE], [-1, NE]], channel_multiplier=1))
            assert jb.n == 3
            with pool.Fori(0, T) as s:
                pool.tensor_copy(A0[:, ds(s * NP, NP)], A1C[:, ds(s * NP, NP)])
            stage_barrier(pool, 2)
            masks = Chain(pool, s_masks)
            masks(pool.memset(bmask, 0.0))
            for h2 in range(2):
                masks(pool.memset(bmask[64 * h2:64 * h2 + 64, 64 * h2:64 * h2 + 64], 1.0))
            masks(pool.iota(iota8, [[1, TK]], base=0, channel_multiplier=0, allow_small_or_imprecise_dtypes=True))
            def gathers(t, k, rows):
                pool.wait_ge(s_rows, t + 1)
                for g in range(GPT):
                    if g == 8:
                        pool.wait_ge(s_mo, T)
                    if g % 4 == 0:
                        pool.wait_ge(s_slot, t * GPT + (g + 4))
                        pool.sem_inc(s_passed[0], 1)
                    pool.indirect_dma_start(slot[g % SLOTS][0:rows, :], None, d["L1_ffn_w"],
                                            bass.IndirectOffsetOnAxis(ap=rowid[k][0:rows, g:g + 1], axis=0)
                                            ).then_inc(s_gat[g % SLOTS], 16)

            with pool.Fori(0, T // 2 - 1) as pair:
                for k in range(2):
                    gathers(pair * 2 + k, k, P)
            gathers(T - 2, 0, P)
            gathers(T - 1, 1, TAIL)
            pool.drain()

        @block.scalar
        def _(act):
            link = Chain(act, s_sc)

            def deviation(l, eps=epsc):
                act.wait_ge(s_var[l], 1)
                var = mv.rearrange("p (t c) -> p t c", c=2)[:, :, 1]
                act.activation(rstd2, var, ACT.Sqrt, bias=eps).then_inc(s_sd[l], 1)

            def transpose_copies(l):
                with act.Fori(0, T // 2) as pair:
                    for k in range(2):
                        act.wait_ge(s_xtp[l], pair * 2 + (k + 1))
                        act.activation(XNT3[:, :, ds((pair * 2 + k) * P, P)],
                                       bank(k).rearrange("p (i c) -> p i c", i=KD), ACT.Copy).then_inc(s_xt[l], 1)

            act.wait_ge(s_const, CONSTANTS)
            deviation(0)
            transpose_copies(0)
            act.wait_ge(s_pe1, 1)
            act.activation(WF, bank(5, 256), ACT.Copy).then_inc(s_mm, 1)
            act.activation(qkb, bank(6, 64, 1), ACT.Copy).then_inc(s_mm, 1)
            for j in range(KD):
                act.wait_ge(s_pe1, 2 + j)
                act.activation(VO[:, 512 * j:512 * j + 512], bank(j), ACT.Copy).then_inc(s_mm, 1)
            with act.Fori(0, T // 2) as pair:
                for k in range(2):
                    act.wait_ge(s_z, pair * 2 + (k + 1))
                    act.activation(ZF[:, ds((pair * 2 + k) * D, D)], bank(k), ACT.Copy).then_inc(s_zc, 1)
            act.wait_ge(s_pe1, 6)
            act.activation(qlT, PS[HR:2 * HR, 1024:1024 + NP], ACT.Copy).then_inc(s_qlc, 1)
            act.wait_ge(s_kneg, 1)
            act.activation(kTe[:, 0:N], PS[0:HR, 1024:1024 + N], ACT.Exp, bias=kneg, accum_out=ksum).then_inc(s_kexp, 1)
            act.wait_ge(s_qsub, 1)
            act.activation(qrow, qrow, ACT.Exp).then_inc(s_qexp, 1)
            stage_barrier(act, 0)
            A1v = A1C.rearrange("p (s n) -> p s n", s=T)
            with act.Fori(0, NW // 2) as pair:
                for k in range(2):
                    w = pair * 2 + k
                    banks = PS[:, 1536 * k:1536 * k + NP].rearrange("p (s c) -> p s c", s=T)
                    act.wait_ge(s_win, w + 1)
                    act.wait_ge(s_stf, w + 1)
                    act.activation(staged[:, 960 * k:960 * k + 960].rearrange("p (s c) -> p s c", s=T),
                                   banks[:, :, 0:96], ACT.Copy).then_inc(s_stg, 1)
                    act.activation(A1v[:, :, ds(w * WIN, WIN)], banks[:, :, 96:128], ACT.Copy).then_inc(s_wevac, 1)
            stage_barrier(act, 1)
            deviation(1)
            transpose_copies(1)
            act.wait_ge(s_pm, 1)
            act.activation(prob[:, 0:N], PS[0:NE, 1024:1024 + N], ACT.Exp, bias=pneg, accum_out=psumc).then_inc(s_pexp, 1)
            act.wait_ge(s_lg, 2)
            act.activation(probR, PS[:, 1024:1024 + NP], ACT.Copy).then_inc(s_pexp, 1)
            act.wait_ge(s_es, 1)
            act.activation(esame, bank(6, P), ACT.Copy).then_inc(s_esc, 1)
            act.wait_ge(s_moew, 32)

            def hidden_layer(e, k):
                for u, (f, (c0, cn)) in enumerate(HIDDEN):
                    act.wait_ge(s_h, e * 6 + (u + 1))
                    act.activation(hT[k][:, f * NP + c0:f * NP + c0 + cn], bank(u % 3, cn), ACT.Gelu,
                                   bias=b1k[k][:, f:f + 1]).then_inc(s_gelu, 1)

            for e in range(2):
                hidden_layer(e, e)
            with act.Fori(1, NE // 2) as pair:
                for k in range(2):
                    act.wait_ge(s_oy, (pair * 2 + k) * T + 1)
                    hidden_layer(pair * 2 + k, k)
            stage_barrier(act, 2)
            deviation(2)
            transpose_copies(2)
            with act.Fori(0, T // 2) as pair:
                for k in range(2):
                    act.wait_ge(s_y, pair * 2 + (k + 1))
                    act.activation(ZF[:, ds((pair * 2 + k) * D, D)], bank(k), ACT.Copy).then_inc(s_yc, 1)
            with act.Fori(0, T) as t:
                act.wait_ge(s_q1s, t + 1)
                act.activation(QR[:, ds(t * D, D)], QR[:, ds(t * D, D)], ACT.Exp).then_inc(s_q1e, 1)
            for j in range(KD):
                act.wait_ge(s_k1m, j + 1)
                act.activation(kT1[:, NP * j:NP * j + N], PS[:, 1536 * (j % 2):1536 * (j % 2) + N], ACT.Exp,
                               bias=kneg1[:, j:j + 1], accum_out=ksum1[:, j:j + 1]).then_inc(s_k1e, 1)
                for t in VALUES_AFTER[j]:
                    act.wait_ge(s_v1, t + 1)
                    act.activation(V1[:, D * t:D * t + D], bank(6 + t % 2), ACT.Copy).then_inc(s_v1c, 1)
            with act.Fori(0, T // 2) as pair:
                for k in range(2):
                    act.wait_ge(s_kr, pair * 2 + (k + 1))
                    act.activation(kR1[:, ds((pair * 2 + k) * D, D)], bank(k), ACT.Copy).then_inc(s_krc, 1)
            qT3 = qT1.rearrange("p (j n) -> p j n", j=KD)
            with act.Fori(0, T // 2) as pair:
                for k in range(2):
                    act.wait_ge(s_qt, pair * 2 + (k + 1))
                    act.activation(qT3[:, :, ds((pair * 2 + k) * P, P)],
                                   bank(k).rearrange("p (j c) -> p j c", j=KD), ACT.Copy).then_inc(s_qtc, 1)
            def head_queries(t, half):
                act.wait_ge(s_q4, t * 2 + (half + 1))
                for h in range(4 * half, 4 * half + 4):
                    act.activation(qT4[:, P * h:P * h + P], bank(half, P, start=P * (h % 4)), ACT.Identity,
                                   bias=bq4[:, h:h + 1]).then_inc(s_q4c, 1)

            def score_exponentials(t, k):
                act.wait_ge(s_sub4, t + 1)
                act.activation(soft[k], soft[k], ACT.Exp).then_inc(s_exp4, 1)

            def up_diagonals(t, k, more, norm):
                for h in range(PH):
                    if norm and h == 2:
                        mixer_deviation(t + 2)
                    if norm and h == 3:
                        stream_deviation(t + 2)
                    if norm and h == 5:
                        norm_transpose(t + 2, k)
                    if norm and h == 7:
                        head_queries(t + 2, 0)
                    if more and h == 7:
                        score_exponentials(t + 1, 1 - k)
                    act.wait_ge(s_vals, t * PH + (h + 1))
                    for g in range(TK * h, TK * h + TK):
                        act.wait_ge(s_slot, t * GPT + (g + 1 + SLOTS - 4))
                        act.activation(diag[g % 4], ident[:, :], ACT.Copy, scale=vals[:, g:g + 1]).then_inc(s_dg, 1)
                if norm:
                    head_queries(t + 2, 1)

            def mixer_output(t):
                act.wait_ge(s_mo, t + 1)
                act.activation(MO[:, D * t:D * t + D], bank(6 + t % 2), ACT.Copy).then_inc(s_moc, 1)

            def mixer_deviation(t):
                act.wait_ge(s_var1, t + 1)
                act.activation(dev1[0], mv1[0][:, 1:2], ACT.Sqrt, bias=epsc).then_inc(s_sd1, 1)

            def stream_deviation(t):
                act.wait_ge(s_var[3], t + 1)
                act.activation(dev1[1], mv1[1][:, 1:2], ACT.Sqrt, bias=epsc).then_inc(s_sd[3], 1)

            def norm_transpose(t, k):
                act.wait_ge(s_xtp[3], t + 1)
                act.activation(XNT3[:, :, ds(t * P, P)], bank(k).rearrange("p (i c) -> p i c", i=KD),
                               ACT.Copy).then_inc(s_xt[3], 1)

            mixer_output(0)
            mixer_deviation(0)
            mixer_output(1)
            stream_deviation(0)
            mixer_output(2)
            norm_transpose(0, 0)
            mixer_deviation(1)
            stream_deviation(1)
            act.wait_ge(s_w4, 48)
            head_queries(0, 0)
            head_queries(0, 1)
            for t in range(3, T):
                mixer_output(t)
            norm_transpose(1, 1)
            head_queries(1, 0)
            head_queries(1, 1)
            score_exponentials(0, 0)
            with act.Fori(0, T // 2 - 1) as pair:
                for k in range(2):
                    up_diagonals(pair * 2 + k, k, True, True)
            up_diagonals(T - 2, 0, True, False)
            up_diagonals(T - 1, 1, False, False)
            act.drain()

        @block.vector
        def _(v):
            link = Chain(v, s_dv)

            def row_statistics(t):
                return v.bn_stats(stat[:, ds(t * 6, 6)], X[:, ds(t * D, D)])

            def deviations(l):
                for t in range(T):
                    last = v.bn_aggr(mv[:, 2 * t:2 * t + 2], stat[:, 6 * t:6 * t + 6])
                last.then_inc(s_var[l], 1)
                v.wait_ge(s_sd[l], 1)
                link(v.reciprocal(rstd, rstd2))

            def normalise(l):
                with v.Fori(0, T) as t:
                    v.tensor_scalar(XN[:, ds(t * D, D)], X[:, ds(t * D, D)], mv[:, ds(t * 2, 1)], rstd[:, ds(t, 1)],
                                    ALU.subtract, ALU.mult).then_inc(s_xn[l], 1)

            v.wait_ge(s_const, CONSTANTS)
            v.wait_ge(s_x, 16)
            for t in range(T):
                last = row_statistics(t)
            link(last)
            deviations(0)
            normalise(0)
            v.wait_ge(s_bo, 1)
            v.wait_ge(s_xn[0], T)
            for t in range(T):
                last = v.tensor_tensor(X[:, D * t:D * t + D], bank(7), X[:, D * t:D * t + D], ALU.add)
            link(last)
            v.wait_ge(s_edges, 48)
            link(v.tensor_copy(dstf, raw_dst))
            v.tensor_copy(srcw, raw_src).then_inc(s_bs, 1)
            link(v.tensor_scalar(dtmp, raw_dst, WIN - 1, None, ALU.bitwise_and))
            v.tensor_copy(dlow, dtmp).then_inc(s_bs, 1)
            v.wait_ge(s_bs, 2)
            link(v.tensor_scalar(dtmp, raw_dst, 5, None, ALU.arith_shift_right))
            link(v.tensor_copy(res1, dtmp))
            link(v.scalar_tensor_tensor(srcw, res1, float(WSTEP), srcw, ALU.mult, ALU.add))
            wp = wparts[:, :].rearrange("p (b q) -> p b q", q=4)
            link(v.tensor_copy(wp[:, :, 0], raw_w))
            link(v.tensor_tensor(res1, raw_w, wp[:, :, 0], ALU.subtract))
            link(v.tensor_copy(wp[:, :, 1], res1))
            link(v.tensor_tensor(res1, res1, wp[:, :, 1], ALU.subtract))
            v.tensor_copy(wp[:, :, 2], res1)
            v.memset(wp[:, :, 3], 1.0)
            v.wait_ge(s_bp, 1)
            dT = bank(2, 384).rearrange("p (c e) -> p c e", c=3)
            link(v.tensor_reduce(blkmin, dT, AX.X, ALU.min))
            link(v.tensor_reduce(blkmax, dT, AX.X, ALU.max))
            for c in range(3):
                v.tensor_scalar(dmin[:, P * c:P * c + P], ident[:, :], blkmin[:, c:c + 1], None, ALU.mult)
                last = v.tensor_scalar(dmax[:, P * c:P * c + P], ident[:, :], blkmax[:, c:c + 1], None, ALU.mult)
            last.then_inc(s_bs, 1)
            v.wait_ge(s_bp, 2)
            hb, bb = hit[:, 0:NB], hitb[:, 0:NB]
            link(v.tensor_scalar(hb, bank(3, NB, NW), winhi, None, ALU.is_le))
            link(v.scalar_tensor_tensor(hb, bank(4, NB, NW), winlo, hb, ALU.is_ge, ALU.mult))
            link(v.tensor_tensor(bb, hb, bup[:, 0:NB], ALU.mult))
            link(v.tensor_reduce(wend, bb, AX.X, ALU.max))
            link(v.tensor_tensor(bb, hb, bdown[:, 0:NB], ALU.mult))
            link(v.tensor_reduce(wfirst, bb, AX.X, ALU.max))
            link(v.tensor_scalar(wfirst, wfirst, -1.0, float(NB), ALU.mult, ALU.add))
            link(v.tensor_scalar(wfirst, wfirst, float(NB - 1), None, ALU.min))
            link(v.scalar_tensor_tensor(wend, wfirst, 1.0, wend, ALU.add, ALU.max))
            link(v.tensor_tensor(wend, wend, wfirst, ALU.subtract))
            v.tensor_scalar(bb[:, 0:TURNS], bthird[:, 0:TURNS], wend, None, ALU.is_lt, ALU.add,
                            accum_out=wcnt).then_inc(s_bs, 1)
            v.wait_ge(s_bp, 3)
            link(v.tensor_copy(woff, bank(5, 1, NW)))
            for c, col in enumerate((wfirst, wcnt, woff)):
                last = v.tensor_scalar(flat3[:, NW * c:NW * c + NW], ident[0:NW, 0:NW], col, None, ALU.mult)
            last.then_inc(s_bs, 1)
            v.wait_ge(s_bp, 4)
            link(v.tensor_copy(bounds3, bank(2, 3 * NW, 1)))
            link(v.tensor_scalar(bounds3[:, NW:2 * NW], bounds3[:, NW:2 * NW], FIRST_BITS, None, ALU.logical_shift_left))
            link(v.tensor_scalar(bounds3[:, 2 * NW:], bounds3[:, 2 * NW:], FIRST_BITS + TURN_BITS, None,
                                 ALU.logical_shift_left))
            link(v.tensor_tensor(bounds, bounds3[:, 0:NW], bounds3[:, NW:2 * NW], ALU.bitwise_or))
            v.tensor_tensor(bounds, bounds, bounds3[:, 2 * NW:], ALU.bitwise_or).then_inc(s_bound, 1)
            def places(first, end):
                n = end - first
                return v.tensor_tensor(eq32[:, WIN * first:WIN * end].rearrange("p (b c) -> p b c", c=WIN),
                                       iota32[:, :].unsqueeze(1).to_broadcast([P, n, WIN]),
                                       dlow[:, first:end].unsqueeze(2).to_broadcast([P, n, WIN]), ALU.is_equal)

            under_win = (4096 - EQ0) // (WIN // 2)
            v.wait_ge(s_pe1, 5)
            places(under_win, NBV)
            qv = qrow.rearrange("p (a r) -> p a r", r=KR)
            qb = qmax.unsqueeze(2).to_broadcast([P, T * HEADS, KR])
            v.wait_ge(s_pe1, 6)
            v.wait_ge(s_qlc, 1)
            v.tensor_reduce(kneg, PS[0:HR, 1024:1024 + N], AX.X, ALU.max, negate=True).then_inc(s_kneg, 1)
            v.memset(kTe[:, N:NP], 0.0).then_inc(s_mm, 1)
            v.wait_ge(s_pe1, 7)
            link(v.tensor_reduce(qmax, bank(6, 320).rearrange("p (a r) -> p a r", r=KR), AX.X, ALU.max))
            v.tensor_tensor(qv, bank(6, 320).rearrange("p (a r) -> p a r", r=KR), qb, ALU.subtract).then_inc(s_qsub, 1)
            v.wait_ge(s_qexp, 1)
            link(v.tensor_reduce(qmax, qv, AX.X, ALU.add))
            link(v.reciprocal(qmax, qmax))
            v.tensor_tensor(qv, qv, qb, ALU.mult).then_inc(s_mm, 1)
            v.wait_ge(s_kexp, 1)
            link(v.reciprocal(ksum, ksum))
            v.wait_ge(s_pe1, 8)
            v.tensor_copy(qTs, PS[0:HR, 1024:1024 + NP]).then_inc(s_mm, 1)
            v.wait_ge(s_pe1, 9)
            v.tensor_copy(krow, bank(6, 320)).then_inc(s_mm, 1)
            v.wait_ge(s_kx, 1)
            v.tensor_copy(kxr, bank(7, 512, HR)).then_inc(s_kxc, 1)
            v.wait_ge(s_pe1, 10)
            v.tensor_copy(kxT, bank(7, 128)).then_inc(s_mm, 1)
            v.wait_ge(s_pe1, 11)
            link(v.tensor_scalar(kxm, bank(5, 512, HR), ksum, None, ALU.mult))
            v.wait_ge(s_pe1, 12)
            link(v.tensor_tensor(kxm, kxm, bank(4, 512, HR), ALU.add))
            v.tensor_tensor(kxm, kxm, headmask, ALU.mult).then_inc(s_mm, 1)
            v.wait_ge(s_pe1, 13)
            v.tensor_copy(kxmT, bank(7, 128)).then_inc(s_mm, 1)
            v.wait_ge(s_pe1, 14)
            v.tensor_copy(Mx, bank(5, 512, HR)).then_inc(s_mm, 1)
            places(0, under_win)
            with v.Fori(0, T // 2) as pair:
                for k in range(2):
                    t = pair * 2 + k
                    v.wait_ge(s_mix, t + 1)
                    v.tensor_tensor(X[:, ds(t * D, D)], bank(k), X[:, ds(t * D, D)], ALU.add).then_inc(s_mixa, 1)
            stage_barrier(v, 0)
            v.memset(zero_b, 0.0).then_inc(s_ohr, 1)
            iw = iota16[:, :]
            v.wait_ge(s_ohr, 1)
            with v.Fori(0, NW) as w:
                begin, end, lower = window_bounds(v, w)
                with v.Fori(begin, end, OHB) as place:
                    for k in range(OHB):
                        b = edge_block(place + k, lower)
                        v.wait_ge(s_ohf, place + (k + 1))
                        v.tensor_scalar(ohs[k], iw, srcw[:, ds(b, 1)], windows[:, ds(w, 1)],
                                        ALU.subtract, ALU.is_equal).then_inc(s_ohr, 1)
            with v.Fori(0, T // 2) as pair:
                link.enter(pair, 2)
                for k in range(2):
                    t = pair * 2 + k
                    v.wait_ge(s_agg, t + 1)
                    v.scalar_tensor_tensor(X[:, ds(t * D, D)], bank(6 + k), 0.0, X[:, ds(t * D, D)],
                                           ALU.max, ALU.add).then_inc(s_agga, 1)
                    v.wait_ge(s_agga, t + 1)
                    link(row_statistics(t))
            link.leave(T // 2)
            stage_barrier(v, 1)
            deviations(1)
            normalise(1)
            v.wait_ge(s_jc, 3)
            link(v.tensor_scalar(jcl, jcol, 3, None, ALU.arith_shift_right))
            link(v.tensor_scalar(jbits[:, 0:1], jcl, 4.0, None, ALU.min))
            link(v.tensor_scalar(jbits[:, 0:1], jbits[:, 0:1], 28, None, ALU.logical_shift_left))
            for r in range(1, ROUNDS):
                link(v.tensor_scalar(jbits[:, r:r + 1], jcl, 28 - 4 * r, None, ALU.logical_shift_left))
            for r in range(ROUNDS):
                link(v.memset(scale2[:, r:r + 1], float(1 << (28 - 4 * r))))
            link(v.memset(basei, 0))
            v.wait_ge(s_lg, 1)
            v.tensor_reduce(pneg, PS[0:NE, 1024:1024 + N], AX.X, ALU.max, negate=True).then_inc(s_pm, 1)
            v.wait_ge(s_pexp, 1)
            link(v.reciprocal(psumc, psumc))
            link(v.memset(prob[:, N:NP], 0.0))
            v.tensor_scalar(prob[:, 0:N], prob[:, 0:N], psumc, None, ALU.mult).then_inc(s_ro, 1)
            v.wait_ge(s_pexp, 2)
            with v.Fori(0, ROUNDS) as r:
                link.enter(r, 5)
                link(v.tensor_tensor(thri, basei, jbits[:, ds(r, 1)], ALU.bitwise_or))
                link(v.tensor_scalar(sel1[:, 0:N], probR[:, 0:N], thrf, None, ALU.is_ge, ALU.add, accum_out=cntc))
                v.tensor_scalar(okc, cntc, float(CAP), None, ALU.is_ge).then_inc(s_ok, 1)
                v.wait_ge(s_oks, r + 1)
                link(v.tensor_scalar(stepf, bank(5, 1), -1.0, scale2[:, ds(r, 1)], ALU.add, ALU.mult))
                link(v.tensor_copy(stepi, stepf))
                link(v.tensor_tensor(basei, basei, stepi, ALU.bitwise_or))
            link.leave(ROUNDS)
            thr8 = basei[0:NE, :].bitcast(F32)
            g8, e8, c8 = sel1[0:NE, 0:N], sel2[0:NE, 0:N], probR[0:NE, 0:N]
            link(v.tensor_scalar(g8, prob[:, 0:N], thr8, None, ALU.is_gt, ALU.add, accum_out=cgt))
            link(v.tensor_scalar(e8, prob[:, 0:N], thr8, None, ALU.is_equal))
            link(v.tensor_tensor_scan(c8, e8, e8, 0.0, ALU.add, ALU.max))
            link(v.tensor_scalar(need, cgt, -1.0, float(CAP), ALU.mult, ALU.add))
            link(v.scalar_tensor_tensor(e8, c8, need, e8, ALU.is_le, ALU.mult))
            link(v.tensor_tensor(g8, g8, e8, ALU.add))
            v.tensor_tensor(prob[:, 0:N], prob[:, 0:N], g8, ALU.mult).then_inc(s_ro, 1)
            v.wait_ge(s_lg, 3)
            link(v.tensor_copy(gate, bank(7, NE * T)))
            v.sem_inc(s_ro, 1)
            for t in range(T):
                v.wait_ge(s_oy, t + 2)
                v.tensor_tensor(X[:, D * t:D * t + D], bank(3 + t % 5), X[:, D * t:D * t + D], ALU.add).then_inc(s_oa, 1)
            with v.Fori(0, NE - 1) as e:
                for t in range(T):
                    v.wait_ge(s_oy, e * T + (T + t + 2))
                    v.scalar_tensor_tensor(X[:, D * t:D * t + D], bank(3 + t % 5), gate[:, ds(e + NE * t, 1)],
                                           X[:, D * t:D * t + D], ALU.mult, ALU.add).then_inc(s_oa, 1)
            for t in range(T):
                v.wait_ge(s_oy, NE * T + (t + 2))
                v.scalar_tensor_tensor(X[:, D * t:D * t + D], bank(3 + t % 5), gate[:, NE * t + NE - 1:NE * t + NE],
                                       X[:, D * t:D * t + D], ALU.mult, ALU.add).then_inc(s_oa, 1)
                v.wait_ge(s_oa, 5 + NE * T + t + 1)
                last = row_statistics(t)
            link(last)
            stage_barrier(v, 2)
            deviations(2)
            normalise(2)
            v.wait_ge(s_xn[2], T)
            v.wait_ge(s_bc, 1)
            link(v.tensor_copy(gam, bank(7)))
            link(v.tensor_copy(alphac, bank(5, 1)))
            link(v.tensor_scalar(ab, bank(6), alphac, None, ALU.mult))
            v.sem_inc(s_bcc, 1)
            v.tensor_reduce(a1sum, A0.rearrange("p (s n) -> p n s", s=T), AX.X, ALU.add).then_inc(s_dsum, 1)
            with v.Fori(0, T) as t:
                xt = X[:, ds(t * D, D)]
                link.enter(t, 2)
                link(v.tensor_tensor(xt, xt, XN[:, ds(t * D, D)], ALU.add))
                link(v.tensor_tensor(xt, xt, ab, ALU.add))
            link.leave(T)
            v.wait_ge(s_deg, 1)
            link(v.tensor_scalar(degc, bank(4, T), 1.0, None, ALU.max))
            link(v.reciprocal(degc, degc))
            link(v.tensor_scalar(adeg, degc, alphac, None, ALU.mult))
            with v.Fori(0, T // 2) as pair:
                for k in range(2):
                    t = pair * 2 + k
                    v.wait_ge(s_agg1, t + 1)
                    v.scalar_tensor_tensor(X[:, ds(t * D, D)], bank(2 + k), adeg[:, ds(t, 1)], X[:, ds(t * D, D)],
                                           ALU.mult, ALU.add).then_inc(s_agga1, 1)
            with v.Fori(0, T // 2) as pair:
                link.enter(pair, 2)
                for k in range(2):
                    t = pair * 2 + k
                    qm = qm1[:, HEADS * k:HEADS * k + HEADS]
                    v.wait_ge(s_q1, t + 1)
                    qp = bank(6 + k).rearrange("p (h c) -> p h c", h=HEADS)
                    link(v.tensor_reduce(qm, qp, AX.X, ALU.max))
                    v.tensor_tensor(QR[:, ds(t * D, D)].rearrange("p (h c) -> p h c", h=HEADS), qp,
                                    qm.unsqueeze(2).to_broadcast([P, HEADS, 64]), ALU.subtract).then_inc(s_q1s, 1)
            link.leave(T // 2)
            for j in range(KD):
                v.wait_ge(s_k1, j + 1)
                v.tensor_reduce(kneg1[:, j:j + 1], PS[:, 1536 * (j % 2):1536 * (j % 2) + N], AX.X, ALU.max,
                                negate=True).then_inc(s_k1m, 1)
            kT3 = kT1.rearrange("p (j n) -> p j n", j=KD)
            v.memset(kT3[:, :, N:NP], 0.0).then_inc(s_k1e, 1)
            with v.Fori(0, T // 2) as pair:
                link.enter(pair, 6)
                for k in range(2):
                    t = pair * 2 + k
                    v.wait_ge(s_q1e, t + 1)
                    qm = qm1[:, HEADS * k:HEADS * k + HEADS]
                    qr = QR[:, ds(t * D, D)].rearrange("p (h c) -> p h c", h=HEADS)
                    link(v.tensor_reduce(qm, qr, AX.X, ALU.add))
                    link(v.reciprocal(qm, qm))
                    link(v.tensor_scalar(qm, qm, 64 ** -0.5, None, ALU.mult))
                    v.tensor_tensor(qr, qr, qm.unsqueeze(2).to_broadcast([P, HEADS, 64]), ALU.mult).then_inc(s_q1n, 1)
            link.leave(T // 2)
            v.wait_ge(s_k1e, KD + 1)
            link(v.reciprocal(ksum1, ksum1))
            v.wait_ge(s_masks, 4)
            v.wait_ge(s_cx, 1)
            v.tensor_tensor(ctxT.rearrange("p (j c) -> p j c", j=KD), bank(2).rearrange("p (j c) -> p j c", j=KD),
                            bmask.unsqueeze(1).to_broadcast([P, KD, P]), ALU.mult).then_inc(s_cxc, 1)
            for j in range(KD):
                v.wait_ge(s_m1, j + 1)
                v.tensor_scalar(M1[:, D * j:D * j + D], bank(3 + j % 2), ksum1[:, j:j + 1], None, ALU.mult).then_inc(s_m1c, 1)
            def mixer_variance(t):
                v.wait_ge(s_moc, t + 1)
                v.sem_inc(s_passed[1], 1)
                link(v.bn_stats(stat1[0], MO[:, ds(t * D, D)]))
                v.sem_inc(s_passed[1], 1)
                v.bn_aggr(mv1[0], stat1[0]).then_inc(s_var1, 1)

            def add_mixed(t):
                mo, x = MO[:, ds(t * D, D)], X[:, ds(t * D, D)]
                v.wait_ge(s_sd1, t + 1)
                link(v.reciprocal(rstd1[0], dev1[0]))
                link(v.scalar_tensor_tensor(mo, mo, mv1[0][:, 0:1], gam, ALU.subtract, ALU.mult))
                link(v.scalar_tensor_tensor(x, mo, rstd1[0], x, ALU.mult, ALU.add))
                v.sem_inc(s_passed[1], 1)
                link(v.bn_stats(stat1[1], x))
                v.sem_inc(s_passed[1], 1)
                v.bn_aggr(mv1[1], stat1[1]).then_inc(s_var[3], 1)

            def normalise_tile(t, k):
                v.wait_ge(s_sd[3], t + 1)
                link(v.reciprocal(rstd1[1], dev1[1]))
                v.tensor_scalar(xnext[k], X[:, ds(t * D, D)], mv1[1][:, 0:1], rstd1[1],
                                ALU.subtract, ALU.mult).then_inc(s_xn[3], 1)

            def head_keys(t, h):
                v.wait_ge(s_sc4, t * PH + (h + 1))
                v.sem_inc(s_passed[1], 1)
                half = [bank(2 + 2 * (h % 2) + c, NK) for c in range(2)]
                cols = [slice(16 * h + 8 * c, 16 * h + 8 * c + 8) for c in range(2)]
                v.max(s8[:, cols[0]], half[0])
                link(v.max(s8[:, cols[1]], half[1]))
                v.sem_inc(s_passed[1], 1)
                v.max_index(i8[:, cols[0]], s8[:, cols[0]], half[0])
                v.max_index(i8[:, cols[1]], s8[:, cols[1]], half[1]).then_inc(s_scf, 1)

            def pair_scores(t):
                v.wait_ge(s_scf, t * PH + (PH + 2))
                s4 = s8.rearrange("p (h c k) -> p h c k", h=PH, c=2)
                c4 = comb.rearrange("p (h a b) -> p h a b", h=PH, a=TK)
                link(v.tensor_tensor(c4, s4[:, :, 0, :].unsqueeze(3).to_broadcast([P, PH, TK, TK]),
                                     s4[:, :, 1, :].unsqueeze(2).to_broadcast([P, PH, TK, TK]), ALU.add))
                v.sem_inc(s_passed[1], 1)
                for h in range(PH):
                    last = v.max(v8[:, 8 * h:8 * h + 8], comb[:, 64 * h:64 * h + 64])
                link(last)
                v.sem_inc(s_passed[1], 1)
                for h in range(PH):
                    last = v.max_index(pos[:, 8 * h:8 * h + 8], v8[:, 8 * h:8 * h + 8], comb[:, 64 * h:64 * h + 64])
                link(last)

            def row_numbers(t, k):
                link(v.tensor_copy(i8f, i8))
                link(v.tensor_scalar(posa, pos, 3, None, ALU.logical_shift_right))
                link(v.tensor_scalar(posb, pos, 7, None, ALU.bitwise_and))
                link(v.tensor_copy(posf[:, 0:64], posa))
                link(v.tensor_copy(posf[:, 64:128], posb))
                i4 = i8f.rearrange("p (h c k) -> p h c k", h=PH, c=2)
                e3 = eqk.rearrange("p (g j) -> p g j", j=TK)
                e4 = eqk.rearrange("p (h k j) -> p h k j", h=PH, k=TK)
                for c in range(2):
                    link(v.tensor_tensor(e3, posf[:, 64 * c:64 * c + 64].unsqueeze(2).to_broadcast([P, 64, TK]),
                                         iota8.unsqueeze(1).to_broadcast([P, 64, TK]), ALU.is_equal))
                    link(v.tensor_tensor(e4, e4, i4[:, :, c, :].unsqueeze(2).to_broadcast([P, PH, TK, TK]), ALU.mult))
                    link(v.tensor_reduce(isel[:, 64 * c:64 * c + 64], e3, AX.X, ALU.add))
                v.scalar_tensor_tensor(rowid[k], isel[:, 0:64], float(NK), isel[:, 64:128],
                                       ALU.mult, ALU.add).then_inc(s_rows, 1)
                sv = soft[k].rearrange("p (h k) -> p h k", h=PH)
                vv = v8.rearrange("p (h k) -> p h k", h=PH)
                v.tensor_tensor(sv, vv, vv[:, :, 0:1].to_broadcast([P, PH, TK]), ALU.subtract).then_inc(s_sub4, 1)

            def score_weights(t, k):
                v.wait_ge(s_exp4, t + 1)
                sv = soft[k].rearrange("p (h k) -> p h k", h=PH)
                link(v.tensor_reduce(smax, sv, AX.X, ALU.add))
                link(v.reciprocal(smax, smax))
                link(v.tensor_tensor(sv, sv, smax.unsqueeze(2).to_broadcast([P, PH, TK]), ALU.mult))
                link(v.tensor_copy(xcur[k], xnext[k]))

            def down_products(t, k, heads, more, norm):
                for h in heads:
                    for g in range(TK * h, TK * h + TK):
                        v.wait_ge(s_gat[g % SLOTS], t * (16 * GPT // SLOTS) + 16 * (g // SLOTS + 1))
                        down = slot[g % SLOTS][:, 0:D]
                        last = v.tensor_tensor_reduce(out=down, in0=xcur[k], in1=down, scale=1.0,
                                                      scalar=0.0, op0=ALU.mult, op1=ALU.add,
                                                      accum_out=inner[:, g:g + 1])
                    link(last)
                    v.scalar_tensor_tensor(vals[:, TK * h:TK * h + TK], inner[:, TK * h:TK * h + TK], 0.0,
                                           soft[k][:, TK * h:TK * h + TK], ALU.max, ALU.mult).then_inc(s_vals, 1)
                    if norm and h == 1:
                        mixer_variance(t + 2)
                    if norm and h == 2:
                        add_mixed(t + 2)
                    if norm and h == 3:
                        normalise_tile(t + 2, k)
                    if more and h < 4:
                        head_keys(t + 1, 2 * h)
                        head_keys(t + 1, 2 * h + 1)
                    if more and h == 4:
                        pair_scores(t + 1)
                    if more and h == 5:
                        row_numbers(t + 1, 1 - k)
                    if more and h == 7:
                        score_weights(t + 1, 1 - k)

            def add_output(t, k):
                v.wait_ge(s_slot, t * GPT + (GPT + SLOTS))
                v.tensor_tensor(X[:, ds(t * D, D)], bank(6 + k), X[:, ds(t * D, D)], ALU.add).then_inc(s_xo, 1)

            for t in range(2):
                mixer_variance(t)
                add_mixed(t)
                normalise_tile(t, t)
            for h in range(PH):
                head_keys(0, h)
            pair_scores(0)
            row_numbers(0, 0)
            v.wait_ge(s_mo, T)
            score_weights(0, 0)
            LINKS = 2 * (PH + PH + 3 + 11 + 4 + 6)
            FIRST, REST = range(1), range(1, PH)
            down_products(0, 0, FIRST, True, True)
            with v.Fori(0, T // 2 - 1) as pair:
                link.enter(pair, LINKS)
                for k in range(2):
                    t = pair * 2 + k
                    down_products(t, k, REST, True, True)
                    down_products(t + 1, 1 - k, FIRST, True, True)
                    add_output(t, k)
            link.leave(T // 2 - 1)
            down_products(T - 2, 0, REST, True, False)
            down_products(T - 1, 1, FIRST, False, False)
            add_output(T - 2, 0)
            down_products(T - 1, 1, REST, False, False)
            add_output(T - 1, 1)

        @block.tensor
        def _(pe):
            mm = pe.matmul

            def transposes(l):
                for t in range(T):
                    pe.wait_ge(s_xn[l], t + 1)
                    if t >= 2:
                        pe.wait_ge(s_xt[l], t - 1)
                    for i in range(KD):
                        last = pe.transpose(bank(t % 2, P, start=P * i), XN[:, t * D + P * i:t * D + P * i + P], ident[:, :])
                    last.then_inc(s_xtp[l], 1)

            pe.wait_ge(s_const, CONSTANTS)
            def bounds_product(step):
                pe.wait_ge(s_bs, 1 + step)
                if step == 1:
                    for c in range(3):
                        last = pe.transpose(bank(2, P, start=P * c), dstf[:, P * c:P * c + P], ident[:, :])
                if step == 2:
                    mm(bank(3, NBP, NW), ones[:, 0:NW], dmin, start=True, stop=True)
                    last = mm(bank(4, NBP, NW), ones[:, 0:NW], dmax, start=True, stop=True)
                if step == 3:
                    last = mm(bank(5, 1, NW), tri, wcnt, start=True, stop=True)
                if step == 4:
                    last = mm(bank(2, 3 * NW, 1), ones[0:NW, 0:1], flat3, start=True, stop=True)
                last.then_inc(s_bp, 1)

            transposes(0)
            pe.wait_ge(s_w0, 16 * 13)
            wf = bank(5, 256).rearrange("p (i q j c) -> p i q j c", i=KD, q=2, j=KD)
            qk = bank(6, 64, 1).rearrange("p (q j c) -> p q j c", q=2, j=KD)
            bq = bdqk.rearrange("p (q c) -> p q c", q=2)
            for j in range(KD):
                for i in range(KD):
                    mm(wf[:, i, :, j, :], WinT[:, 512 * j + P * i:512 * j + P * i + P], bq, start=True, stop=True)
                last = mm(qk[:, :, j, :], binc[:, j:j + 1], bq, start=True, stop=True)
            last.then_inc(s_pe1, 1)
            mm(bank(7), ones[0:1, 0:P], boutr, start=True, stop=True).then_inc(s_bo, 1)
            pe.wait_ge(s_xt[0], T)
            for j in range(KD):
                mm(bank(j), bdv, Wout[:, 512 * j:512 * j + 512], start=True, stop=True).then_inc(s_pe1, 1)
            pe.wait_ge(s_mm, 2 + 4)
            for t in range(T):
                if t % 2 == 0 and t > 0:
                    bounds_product(t // 2)
                if t >= 2:
                    pe.wait_ge(s_zc, t - 1)
                for i in range(KD):
                    last = mm(bank(t % 2), XNT3[:, i, P * t:P * t + P], W0[:, 512 * i:512 * i + 512],
                              start=i == 0, stop=i == KD - 1)
                last.then_inc(s_z, 1)
            pe.wait_ge(s_bound, 1)
            for c, (c0, cn) in enumerate(CHUNKS):
                for i in range(KD):
                    mm(bank(2 + c, cn, 2 * HR), WF[:, 64 * i:64 * i + 64], XNT3[:, i, c0:c0 + cn],
                       start=i == 0, stop=False)
                for a in range(0, cn, P):
                    last = mm(bank(2 + c, P, 2 * HR, start=a), qkb[:, 0:64], ones[0:1, 0:P], start=False, stop=a == cn - P)
            last.then_inc(s_pe1, 1)
            pe.wait_ge(s_qlc, 1)
            for t in range(T):
                last = pe.transpose(bank(6, HR, start=HR * t), qlT[:, P * t:P * t + P], ident[HR:2 * HR, HR:2 * HR])
            last.then_inc(s_pe1, 1)
            pe.wait_ge(s_mm, 8)
            pe.wait_ge(s_kexp, 1)
            for t in range(T):
                last = pe.transpose(PS[0:HR, 1024 + P * t:1024 + P * t + P], qrow[:, HR * t:HR * t + HR], ident[:, :])
            last.then_inc(s_pe1, 1)
            for t in range(T):
                last = pe.transpose(bank(6, HR, start=HR * t), kTe[:, P * t:P * t + P], ident[0:HR, 0:HR])
            last.then_inc(s_pe1, 1)
            pe.wait_ge(s_mm, 10)
            for t in range(T):
                last = mm(bank(7, 512, HR), krow[:, HR * t:HR * t + HR], XN[:, t * D:t * D + D],
                          start=t == 0, stop=t == T - 1)
            last.then_inc(s_kx, 1)
            pe.wait_ge(s_kxc, 1)
            for i in range(KD):
                last = pe.transpose(bank(7, HR, start=HR * i), kxr[:, P * i:P * i + P], ident[0:HR, 0:HR])
            last.then_inc(s_pe1, 1)
            pe.wait_ge(s_mm, 11)
            for i in range(KD):
                last = mm(bank(5, 512, HR), kxT[:, HR * i:HR * i + HR], Win[:, 512 * i:512 * i + 512],
                          start=i == 0, stop=i == KD - 1)
            last.then_inc(s_pe1, 1)
            mm(bank(4, 512, HR), ones[0:1, 0:HR], binr, start=True, stop=True).then_inc(s_pe1, 1)
            pe.wait_ge(s_mm, 12)
            for j in range(KD):
                last = pe.transpose(bank(7, HR, start=HR * j), kxm[:, P * j:P * j + P], ident[0:HR, 0:HR])
            last.then_inc(s_pe1, 1)
            pe.wait_ge(s_mm, 13)
            for j in range(KD):
                last = mm(bank(5, 512, HR), kxmT[:, HR * j:HR * j + HR], VO[:, 512 * j:512 * j + 512],
                          start=j == 0, stop=j == KD - 1)
            last.then_inc(s_pe1, 1)
            pe.wait_ge(s_mm, 14)
            pe.wait_ge(s_zc, T)
            for t in range(T):
                if t >= 2:
                    pe.wait_ge(s_mixa, t - 1)
                mm(bank(t % 2), qTs[:, P * t:P * t + P], Mx, start=True, stop=True).then_inc(s_mix, 1)
            stage_barrier(pe, 0)
            pe.sem_inc(s_ohf, OHB)
            pe.sem_inc(s_stf, 2)
            pe.sem_inc(s_wevac, 2)
            pe.wait_ge(s_ohr, 1)
            with pe.Fori(0, NW // 2) as pair:
                for k in range(2):
                    w = pair * 2 + k
                    begin, end, lower = window_bounds(pe, w)
                    pe.wait_ge(s_wevac, w + 1)
                    for b3 in range(3):
                        mm(bank(3 * k + b3, P), zero_b, zero_b, start=True, stop=False, skip_group_check=True)
                    with pe.Fori(begin, end, OHB) as place:
                        for o in range(OHB):
                            pe.wait_ge(s_ohr, place + (o + 2))
                            pe.wait_ge(s_odr, place + (o + 1))
                            for s in range(T):
                                last = mm(PS[:, 1536 * k + P * s:1536 * k + P * s + P], ohs[o][:, P * s:P * s + P],
                                          ohd[o], start=False, stop=False, skip_group_check=True)
                            last.then_inc(s_ohf, 1)
                    for b3 in range(3):
                        last = mm(bank(3 * k + b3, P), zero_b, zero_b, start=False, stop=True, skip_group_check=True)
                    last.then_inc(s_win, 1)
            pe.wait_ge(s_stf, NW + 2)
            for t in range(T):
                if t >= 2:
                    pe.wait_ge(s_agga, t - 1)
                for s in range(T):
                    last = mm(bank(6 + t % 2), A0[:, NP * s + P * t:NP * s + P * t + P], ZF[:, D * s:D * s + D],
                              start=s == 0, stop=s == T - 1)
                last.then_inc(s_agg, 1)
            stage_barrier(pe, 1)
            transposes(1)
            pe.wait_ge(s_xt[1], T)
            pe.wait_ge(s_moew, 32)
            for c, (c0, cn) in enumerate(CHUNKS):
                for i in range(KD):
                    last = mm(bank(2 + c, cn, NE), wr[:, NE * i:NE * i + NE], XNT3[:, i, c0:c0 + cn],
                              start=i == 0, stop=i == KD - 1)
            last.then_inc(s_lg, 1)
            pe.wait_ge(s_ro, 1)
            pe.wait_ge(s_jc, 3)
            for c, (c0, cn) in enumerate(CHUNKS):
                last = mm(bank(2 + c, cn), erep, prob[:, c0:c0 + cn], start=True, stop=True)
            last.then_inc(s_lg, 1)
            mm(bank(6, P), erep, erep, start=True, stop=True).then_inc(s_es, 1)

            def hidden_product(e, k, turn, u):
                f, (c0, cn) = HIDDEN[u]
                pe.wait_ge(s_ew1[k], turn * 32 + 32)
                pe.wait_ge(s_gelu, e * 6 + (u + 1))
                for i in range(KD):
                    last = mm(bank(u % 3, cn), EW[k][:, FF * i + P * f:FF * i + P * f + P],
                              XNT3[:, i, c0:c0 + cn], start=i == 0, stop=i == KD - 1)
                last.then_inc(s_h, 1)

            def hidden(e, k, turn):
                for u in range(len(HIDDEN)):
                    hidden_product(e, k, turn, u)

            pe.wait_ge(s_pexp, 2)
            pe.wait_ge(s_esc, 1)
            pe.sem_inc(s_oa, 5)
            pe.sem_inc(s_gelu, 3)
            pe.sem_inc(s_oy, 1)
            for r in range(ROUNDS):
                pe.wait_ge(s_ok, r + 1)
                mm(bank(5, 1), esame, okc, start=True, stop=True).then_inc(s_oks, 1)
                if r < len(HIDDEN):
                    hidden_product(0, 0, 0, r)
            for u in range(3):
                hidden_product(1, 1, 0, u)
            pe.wait_ge(s_ro, 2)
            for t in range(T):
                last = pe.transpose(bank(7, NE, start=NE * t), prob[:, P * t:P * t + P], ident[0:NE, 0:NE])
            last.then_inc(s_lg, 1)
            for u in range(3, len(HIDDEN)):
                hidden_product(1, 1, 0, u)
            pe.wait_ge(s_ro, 3)
            for t in range(T):
                pe.wait_ge(s_oa, t + 1)
                mm(bank(3 + t % 5), prob[:, P * t:P * t + P], b2, start=True, stop=True).then_inc(s_oy, 1)

            def expert_output(e, k, turn):
                pe.wait_ge(s_gelu, e * 6 + 9)
                pe.wait_ge(s_ew2[k], turn * 16 + 16)
                for t in range(T):
                    pe.wait_ge(s_oa, e * T + (T + t + 1))
                    for f in range(FB):
                        last = mm(bank(3 + t % 5), hT[k][:, NP * f + P * t:NP * f + P * t + P],
                                  EW[k][:, 1024 + D * f:1024 + D * f + D], start=f == 0, stop=f == FB - 1)
                    last.then_inc(s_oy, 1)

            with pe.Fori(0, NE // 2 - 1) as pair:
                for k in range(2):
                    expert_output(pair * 2 + k, k, pair)
                    hidden(pair * 2 + (k + 2), k, pair + 1)
            for k in range(2):
                expert_output(NE - 2 + k, k, NE // 2 - 1)
            stage_barrier(pe, 2)
            pe.wait_ge(s_w1, 16 * 4)
            mm(bank(7), ones[0:1, 0:P], gamr, start=True, stop=True)
            mm(bank(6), ones[0:1, 0:P], br1, start=True, stop=True)
            mm(bank(5, 1), ones[0:1, 0:P], alr, start=True, stop=True).then_inc(s_bc, 1)
            transposes(2)
            pe.wait_ge(s_xt[2], T)
            for t in range(T):
                if t >= 2:
                    pe.wait_ge(s_yc, t - 1)
                for i in range(KD):
                    last = mm(bank(t % 2), XNT3[:, i, P * t:P * t + P], Wg1[:, D * i:D * i + D],
                              start=i == 0, stop=i == KD - 1)
                last.then_inc(s_y, 1)
            pe.wait_ge(s_dsum, 1)
            for t in range(T):
                last = mm(bank(4, 1, start=t), a1sum[:, P * t:P * t + P], ones[:, 0:1], start=True, stop=True)
            last.then_inc(s_deg, 1)
            pe.wait_ge(s_yc, T)
            for t in range(T):
                if t >= 2:
                    pe.wait_ge(s_agga1, t - 1)
                for s in range(T):
                    last = mm(bank(2 + t % 2), A0[:, NP * s + P * t:NP * s + P * t + P], ZF[:, D * s:D * s + D],
                              start=s == 0, stop=s == T - 1)
                last.then_inc(s_agg1, 1)
            pe.wait_ge(s_bcc, 1)
            pe.wait_ge(s_w1m, 32)
            Wq3 = Wqkv.rearrange("p (i n) -> p i n", i=KD)
            for t in range(T):
                if t >= 2:
                    pe.wait_ge(s_q1s, t - 1)
                for i in range(KD):
                    last = mm(bank(6 + t % 2), XNT3[:, i, P * t:P * t + P], Wq3[:, i, 0:D],
                              start=i == 0, stop=i == KD - 1)
                last.then_inc(s_q1, 1)
            pe.wait_ge(s_agga1, T)
            pe.wait_ge(s_q1s, T)
            for j in range(KD):
                if j >= 2:
                    pe.wait_ge(s_k1e, j)
                for c, (c0, cn) in enumerate(CHUNKS):
                    for i in range(KD):
                        last = mm(bank(3 * (j % 2) + c, cn), Wq3[:, i, D + P * j:D + P * j + P],
                                  XNT3[:, i, c0:c0 + cn], start=i == 0, stop=i == KD - 1)
                last.then_inc(s_k1, 1)
                for t in VALUES_AFTER[j]:
                    if t >= 2:
                        pe.wait_ge(s_v1c, t - 1)
                    for i in range(KD):
                        last = mm(bank(6 + t % 2), XNT3[:, i, P * t:P * t + P], Wq3[:, i, 2 * D:3 * D],
                                  start=i == 0, stop=i == KD - 1)
                    last.then_inc(s_v1, 1)
            pe.wait_ge(s_k1e, KD + 1)
            for t in range(T):
                if t >= 2:
                    pe.wait_ge(s_krc, t - 1)
                for j in range(KD):
                    last = pe.transpose(bank(t % 2, P, start=P * j), kT1[:, NP * j + P * t:NP * j + P * t + P], ident[:, :])
                last.then_inc(s_kr, 1)
            pe.wait_ge(s_krc, T)
            pe.wait_ge(s_v1c, T)
            for j in range(KD):
                for t in range(T):
                    last = mm(bank(2, P, start=P * j), V1[:, D * t + P * j:D * t + P * j + P],
                              kR1[:, D * t + P * j:D * t + P * j + P], start=t == 0, stop=t == T - 1)
            last.then_inc(s_cx, 1)
            pe.wait_ge(s_cxc, 1)
            for j in range(KD):
                if j >= 2:
                    pe.wait_ge(s_m1c, j - 1)
                mm(bank(3 + j % 2), ctxT[:, P * j:P * j + P], Wo1[:, D * j:D * j + D],
                   start=True, stop=True).then_inc(s_m1, 1)
            pe.wait_ge(s_q1n, T)
            for t in range(T):
                if t >= 2:
                    pe.wait_ge(s_qtc, t - 1)
                for j in range(KD):
                    last = pe.transpose(bank(t % 2, P, start=P * j), QR[:, D * t + P * j:D * t + P * j + P], ident[:, :])
                last.then_inc(s_qt, 1)
            pe.wait_ge(s_qtc, T)
            pe.wait_ge(s_m1c, KD)
            pe.sem_inc(s_scf, 2)
            pe.sem_inc(s_slot, SLOTS)

            def mixer_output(t):
                if t >= 2:
                    pe.wait_ge(s_moc, t - 1)
                for j in range(KD):
                    last = mm(bank(6 + t % 2), qT1[:, NP * j + P * t:NP * j + P * t + P], M1[:, D * j:D * j + D],
                              start=j == 0, stop=j == KD - 1)
                last.then_inc(s_mo, 1)

            def norm_transpose(t, k):
                pe.wait_ge(s_xn[3], t + 1)
                for i in range(KD):
                    last = pe.transpose(bank(k, P, start=P * i), xnext[k][:, P * i:P * i + P], ident[:, :])
                last.then_inc(s_xtp[3], 1)

            def queries(t, half):
                for h in range(4 * half, 4 * half + 4):
                    for i in range(KD):
                        last = mm(bank(half, P, start=P * (h % 4)), Wq4[:, 1024 * i + P * h:1024 * i + P * h + P],
                                  XNT3[:, i, ds(t * P, P)], start=i == 0, stop=i == KD - 1)
                last.then_inc(s_q4, 1)

            def scores(t, h):
                pe.wait_ge(s_q4c, t * PH + (h + 1))
                pe.wait_ge(s_scf, t * PH + (h + 1))
                for c in range(2):
                    rows = slice(64 * c, 64 * c + 64)
                    last = mm(bank(2 + 2 * (h % 2) + c, NK), qT4[rows, P * h:P * h + P],
                              keysT[rows, NK * h:NK * h + NK], start=True, stop=True)
                last.then_inc(s_sc4, 1)

            def up_products(t, k, more, norm):
                for h in range(PH):
                    if more and h < 4:
                        scores(t + 1, 2 * h)
                        scores(t + 1, 2 * h + 1)
                    if norm and h == 5:
                        norm_transpose(t + 2, k)
                    if norm and h == 6:
                        pe.wait_ge(s_xt[3], t + 3)
                        queries(t + 2, 0)
                    if norm and h == 7:
                        queries(t + 2, 1)
                    for g in range(TK * h, TK * h + TK):
                        pe.wait_ge(s_dg, t * GPT + (g + 1))
                        last = mm(bank(6 + k), diag[g % 4], slot[g % SLOTS][:, D:2 * D],
                                  start=g == 0, stop=g == GPT - 1)
                        last.then_inc(s_slot, 1)

            for t in range(3):
                mixer_output(t)
            norm_transpose(0, 0)
            pe.wait_ge(s_xt[3], 1)
            pe.wait_ge(s_w4, 48)
            queries(0, 0)
            queries(0, 1)
            for h in range(PH):
                scores(0, h)
                if h in (1, 3, 5):
                    mixer_output(3 + h // 2)
            for t in range(6, T):
                mixer_output(t)
            pe.wait_ge(s_q4c, PH)
            norm_transpose(1, 1)
            pe.wait_ge(s_xt[3], 2)
            queries(1, 0)
            queries(1, 1)
            with pe.Fori(0, T // 2 - 1) as pair:
                for k in range(2):
                    up_products(pair * 2 + k, k, True, True)
            up_products(T - 2, 0, True, False)
            up_products(T - 1, 1, False, False)


_OUT = (N, D)


def _layout(inputs):
    import numpy as np
    a = {k: np.asarray(v) for k, v in inputs.items()}
    pad = NBP * P - EDGES

    def edges(e, fill):
        e = np.concatenate([e, np.full(pad, fill, e.dtype)])
        return np.ascontiguousarray(e.reshape(NBP, P).T)

    x = np.concatenate([a["x"], np.zeros((NP - N, D), a["x"].dtype)])
    got = {
        "x": x,
        "src": edges(a["src"], NP - 1), "dst": edges(a["dst"], NP - 1),
        "edge_weight": edges(a["edge_weight"], 0),
        "L0_gnn_W": a["L0_gnn_W"], "L0_mix_W_in": a["L0_mix_W_in"], "L0_mix_W_in_T": a["L0_mix_W_in"].T,
        "L0_mix_W_q": a["L0_mix_W_q"], "L0_mix_W_k": a["L0_mix_W_k"], "L0_mix_W_v_T": a["L0_mix_W_v"].T,
        "L0_mix_W_out": a["L0_mix_W_out"], "L0_mix_b_in": a["L0_mix_b_in"],
        "L0_ffn_Wr": a["L0_ffn_Wr"].reshape(KD, P, NE).transpose(1, 0, 2).reshape(P, KD * NE),
        "L0_ffn_b1_col": a["L0_ffn_b1"].reshape(NE * FB, P).T, "L0_ffn_b2": a["L0_ffn_b2"],
        "L0_ffn_W1": a["L0_ffn_W1"], "L0_ffn_W2": a["L0_ffn_W2"],
        "L1_gnn_W_T": a["L1_gnn_W"].T, "L1_gnn_b": a["L1_gnn_b"], "L1_gnn_alpha": a["L1_gnn_alpha"].reshape(1),
        "L1_mix_w_qkv_T": a["L1_mix_w_qkv"].T, "L1_mix_w_out_T": a["L1_mix_w_out"].T, "L1_mix_gamma": a["L1_mix_gamma"],
        "L1_ffn_Wq": a["L1_ffn_Wq"], "L1_ffn_bq_col": a["L1_ffn_bq"].reshape(PH, P).T,
        "L1_ffn_keys_T": a["L1_ffn_keys"].transpose(0, 1, 3, 2).reshape(PH, P, NK),
        "L1_ffn_w": np.concatenate([a["L1_ffn_w_down"], a["L1_ffn_w_up"]], axis=1),
        "L0_mix_b_in_col": a["L0_mix_b_in"].reshape(KD, P).T, "L0_mix_b_out": a["L0_mix_b_out"],
    }
    return {k: np.ascontiguousarray(v) for k, v in got.items()}


def kernel(**inputs):
    import concourse.bacc as _bacc
    from concourse.bass_utils import run_bass_kernel_spmd as _run

    nc = _bacc.Bacc("TRN2", target_bir_lowering=False, num_devices=1)
    arrays, aps = {}, {}
    for name, a in _layout(inputs).items():
        arrays[f"in_{name}_dram"] = a
        aps[name] = nc.dram_tensor(f"in_{name}_dram", a.shape, mybir.dt.from_np(a.dtype), kind="ExternalInput").ap()
    out = nc.dram_tensor("out_0_dram", _OUT, F32, kind="ExternalOutput").ap()
    gps_two_layers(nc, aps, out)
    r = _run(nc, [arrays], core_ids=[0])
    return r.results[0]["out_0_dram"]
```
